# Optimizing a Trainium2 kernel written in Bass

```python
import numpy as np
import jax
import jax.numpy as jnp

def _softmax(x, axis=-1):
    return jax.nn.softmax(x, axis=axis)

def _gelu(x):
    return jax.nn.gelu(x, approximate=True)

def _silu(x):
    return jax.nn.silu(x)

def _sigmoid(x):
    return jax.nn.sigmoid(x)

def _layernorm(x, axis=-1, eps=1e-05):
    m = jnp.mean(x, axis=axis, keepdims=True)
    v = jnp.var(x, axis=axis, keepdims=True)
    return (x - m) / jnp.sqrt(v + eps)

def _scatter_add(tgt, idx, src, axis=0):
    return tgt.at[idx].add(src)

def _segment_sum(src, seg, n):
    return jax.ops.segment_sum(src, seg, n)
kernel_name = 'mk_flamingo_gated_d1_seqx_r8_a1e227'

def setup_inputs(seed: int=0):
    np.random.seed(seed)
    _w = jnp.asarray

    def _rec_inputs():
        import jax
        import jax.numpy as jnp
        _rk = jax.random.key(seed)
        x = -0.0002928 + 1 * jax.random.normal(jax.random.fold_in(_rk, 1), (16, 128, 128), jnp.float32)
        _lenS = 128 - jax.random.randint(jax.random.fold_in(_rk, 7), (16,), 0, max(1, 128 // 4) + 1, jnp.int32)
        _lenS2 = 128 - jax.random.randint(jax.random.fold_in(_rk, 8), (16,), 0, max(1, 128 // 4) + 1, jnp.int32)
        _ctx_1024P = jax.random.normal(jax.random.fold_in(_rk, 11), (16, 16, 128), jnp.float32)
        _ctx_1024c = jax.random.dirichlet(jax.random.fold_in(_rk, 511), 0.3 * jnp.ones((16,), jnp.float32), (16, 128))
        _ctx_1024t = jnp.einsum('bsk,bkd->bsd', _ctx_1024c, _ctx_1024P)
        _ctx_1024t = _ctx_1024t * jax.lax.rsqrt(jnp.mean(jnp.square(_ctx_1024t)) + 1e-12) * 0.953939
        ctx_1024 = -1.39393e-06 + 0.999914 * (_ctx_1024t + 0.3 * jax.random.normal(jax.random.fold_in(_rk, 611), (16, 128, 128), jnp.float32))
        _validS = jnp.arange(128)[None, :] < _lenS[:, None]
        _validS2 = jnp.arange(128)[None, :] < _lenS2[:, None]
        _causal = jnp.tril(jnp.ones((128, 128), dtype=bool))
        mask_Bx1xSxS2_ik0 = jnp.where(jnp.broadcast_to(_validS2[:, None, None, :], (16, 1, 128, 128)), 0, 1).astype(jnp.int32)
        _g = jax.random.normal(jax.random.fold_in(_rk, 9001), (2, 1), jnp.float32)
        _g = jnp.sign(_g) * jnp.maximum(jnp.abs(_g), 1.0) + (_g == 0) * 1.0
        g_xattn = _g[0]
        g_ffn = _g[1]
        return (x, ctx_1024, mask_Bx1xSxS2_ik0, g_xattn, g_ffn)
    x, ctx_1024, mask_Bx1xSxS2_ik0, g_xattn, g_ffn = _rec_inputs()

    def _L0_xattn_setup():
        import jax, jax.numpy as jnp
        import numpy as np
        D_MODEL = 128
        H = 16
        D_K = D_MODEL // H
        B = 2
        S = 256

        def _split_heads(x):
            b, s, _ = x.shape
            return x.reshape(b, s, H, D_K).transpose(0, 2, 1, 3)
        key = jax.random.key(seed)
        ks = jax.random.split(key, 11)
        scale = 1.0 / np.sqrt(D_MODEL)
        inp = {'query': jax.random.normal(ks[0], (B, S, D_MODEL), jnp.float32), 'key_in': jax.random.normal(ks[1], (B, S, D_MODEL), jnp.float32), 'value': jax.random.normal(ks[2], (B, S, D_MODEL), jnp.float32), 'mask': jnp.tril(jnp.ones((S, S), jnp.int32))[None, None, :, :].repeat(B, axis=0), 'w_q': jax.random.normal(ks[3], (D_MODEL, D_MODEL), jnp.float32) * scale, 'b_q': jax.random.normal(ks[4], (D_MODEL,), jnp.float32) * 0.01, 'w_k': jax.random.normal(ks[5], (D_MODEL, D_MODEL), jnp.float32) * scale, 'b_k': jax.random.normal(ks[6], (D_MODEL,), jnp.float32) * 0.01, 'w_v': jax.random.normal(ks[7], (D_MODEL, D_MODEL), jnp.float32) * scale, 'b_v': jax.random.normal(ks[8], (D_MODEL,), jnp.float32) * 0.01, 'w_out': jax.random.normal(ks[9], (D_MODEL, D_MODEL), jnp.float32) * scale, 'b_out': jax.random.normal(ks[10], (D_MODEL,), jnp.float32) * 0.01}
        return inp
    _L0_xattn_all = _L0_xattn_setup()
    _L0_xattn_in = {k: v for k, v in _L0_xattn_all.items() if k in ('w_q', 'b_q', 'w_k', 'b_k', 'w_v', 'b_v', 'w_out', 'b_out')}
    del _L0_xattn_all

    def _L0_ffn_setup():
        import jax, jax.numpy as jnp
        import numpy as np
        from jax import lax
        D = 128
        H = 176
        E = 8
        K = 2
        ROUTER_SCALE = 1.0

        def _expert(x, w1, b1, w3, b3, w2, b2):
            h = jax.nn.silu((x @ w1 + b1) * (x @ w3 + b3))
            return h @ w2 + b2
        key = jax.random.key(seed)
        ks = jax.random.split(key, 16)
        s = 0.02
        inp = {'x': jax.random.normal(ks[0], (2, 256, D), dtype=jnp.float32), 'gate_w': jax.random.normal(ks[1], (E, D), dtype=jnp.float32) * s, 'gate_b': jax.random.normal(ks[2], (E,), dtype=jnp.float32) * s, 'w1': jax.random.normal(ks[3], (E, D, H), dtype=jnp.float32) * s, 'b1': jax.random.normal(ks[4], (E, H), dtype=jnp.float32) * s, 'w3': jax.random.normal(ks[5], (E, D, H), dtype=jnp.float32) * s, 'b3': jax.random.normal(ks[6], (E, H), dtype=jnp.float32) * s, 'w2': jax.random.normal(ks[7], (E, H, D), dtype=jnp.float32) * s, 'b2': jax.random.normal(ks[8], (E, D), dtype=jnp.float32) * s, 'sw1': jax.random.normal(ks[9], (D, H), dtype=jnp.float32) * s, 'sb1': jax.random.normal(ks[10], (H,), dtype=jnp.float32) * s, 'sw3': jax.random.normal(ks[11], (D, H), dtype=jnp.float32) * s, 'sb3': jax.random.normal(ks[12], (H,), dtype=jnp.float32) * s, 'sw2': jax.random.normal(ks[13], (H, D), dtype=jnp.float32) * s, 'sb2': jax.random.normal(ks[14], (D,), dtype=jnp.float32) * s}
        return inp
    _L0_ffn_all = _L0_ffn_setup()
    _L0_ffn_in = {k: v for k, v in _L0_ffn_all.items() if k in ('gate_w', 'gate_b', 'w1', 'b1', 'w3', 'b3', 'w2', 'b2', 'sw1', 'sb1', 'sw3', 'sb3', 'sw2', 'sb2')}
    del _L0_ffn_all
    return {'x': x, 'ctx_1024': ctx_1024, 'mask_Bx1xSxS2_ik0': mask_Bx1xSxS2_ik0, 'g_xattn': g_xattn, 'g_ffn': g_ffn, 'L0_xattn_w_q': _L0_xattn_in['w_q'], 'L0_xattn_b_q': _L0_xattn_in['b_q'], 'L0_xattn_w_k': _L0_xattn_in['w_k'], 'L0_xattn_b_k': _L0_xattn_in['b_k'], 'L0_xattn_w_v': _L0_xattn_in['w_v'], 'L0_xattn_b_v': _L0_xattn_in['b_v'], 'L0_xattn_w_out': _L0_xattn_in['w_out'], 'L0_xattn_b_out': _L0_xattn_in['b_out'], 'L0_ffn_gate_w': _L0_ffn_in['gate_w'], 'L0_ffn_gate_b': _L0_ffn_in['gate_b'], 'L0_ffn_w1': _L0_ffn_in['w1'], 'L0_ffn_b1': _L0_ffn_in['b1'], 'L0_ffn_w3': _L0_ffn_in['w3'], 'L0_ffn_b3': _L0_ffn_in['b3'], 'L0_ffn_w2': _L0_ffn_in['w2'], 'L0_ffn_b2': _L0_ffn_in['b2'], 'L0_ffn_sw1': _L0_ffn_in['sw1'], 'L0_ffn_sb1': _L0_ffn_in['sb1'], 'L0_ffn_sw3': _L0_ffn_in['sw3'], 'L0_ffn_sb3': _L0_ffn_in['sb3'], 'L0_ffn_sw2': _L0_ffn_in['sw2'], 'L0_ffn_sb2': _L0_ffn_in['sb2']}

def reference(x, ctx_1024, mask_Bx1xSxS2_ik0, g_xattn, g_ffn, L0_xattn_w_q, L0_xattn_b_q, L0_xattn_w_k, L0_xattn_b_k, L0_xattn_w_v, L0_xattn_b_v, L0_xattn_w_out, L0_xattn_b_out, L0_ffn_gate_w, L0_ffn_gate_b, L0_ffn_w1, L0_ffn_b1, L0_ffn_w3, L0_ffn_b3, L0_ffn_w2, L0_ffn_b2, L0_ffn_sw1, L0_ffn_sb1, L0_ffn_sw3, L0_ffn_sb3, L0_ffn_sw2, L0_ffn_sb2):
    import jax
    import jax.numpy as jnp

    def _L0_xattn_ref(query, key_in, value, mask, w_q, b_q, w_k, b_k, w_v, b_v, w_out, b_out):
        import jax, jax.numpy as jnp
        import numpy as np
        D_MODEL = 128
        H = 16
        D_K = D_MODEL // H
        B = 2
        S = 256

        def _split_heads(x):
            b, s, _ = x.shape
            return x.reshape(b, s, H, D_K).transpose(0, 2, 1, 3)
        q = _split_heads(query @ w_q.T + b_q)
        k = _split_heads(key_in @ w_k.T + b_k)
        v = _split_heads(value @ w_v.T + b_v)
        scores = jnp.einsum('bhqd,bhkd->bhqk', q, k) / jnp.sqrt(jnp.float32(D_K))
        scores = jnp.where(mask == 0, jnp.float32(-1000000000.0), scores)
        attn = jax.nn.softmax(scores, axis=-1)
        out = jnp.einsum('bhqk,bhkd->bhqd', attn, v)
        out = out.transpose(0, 2, 1, 3).reshape(query.shape[0], -1, D_MODEL)
        return out @ w_out.T + b_out

    def _L0_ffn_ref(x, gate_w, gate_b, w1, b1, w3, b3, w2, b2, sw1, sb1, sw3, sb3, sw2, sb2):
        import jax, jax.numpy as jnp
        import numpy as np
        from jax import lax
        D = 128
        H = 176
        E = 8
        K = 2
        ROUTER_SCALE = 1.0

        def _expert(x, w1, b1, w3, b3, w2, b2):
            h = jax.nn.silu((x @ w1 + b1) * (x @ w3 + b3))
            return h @ w2 + b2
        shape = x.shape
        xf = x.reshape(-1, D)
        T = xf.shape[0]
        scores = jax.nn.softmax(xf @ gate_w.T, axis=-1)
        biased = scores + gate_b
        _, idx = lax.top_k(biased, K)
        w = jnp.take_along_axis(scores, idx, axis=-1) * ROUTER_SCALE
        rw = jnp.zeros((T, E), dtype=xf.dtype).at[jnp.arange(T)[:, None], idx].add(w)
        h = jax.nn.silu((jnp.einsum('td,edh->teh', xf, w1) + b1) * (jnp.einsum('td,edh->teh', xf, w3) + b3))
        oe = jnp.einsum('teh,ehd->ted', h, w2) + b2
        y = jnp.einsum('te,ted->td', rw, oe)
        z = _expert(xf, sw1, sb1, sw3, sb3, sw2, sb2)
        return (y + z).reshape(shape)
    x = x + jnp.tanh(g_xattn[0]) * _L0_xattn_ref(_layernorm(x, axis=-1), ctx_1024, ctx_1024, mask_Bx1xSxS2_ik0, L0_xattn_w_q, L0_xattn_b_q, L0_xattn_w_k, L0_xattn_b_k, L0_xattn_w_v, L0_xattn_b_v, L0_xattn_w_out, L0_xattn_b_out)
    x = x + jnp.tanh(g_ffn[0]) * _L0_ffn_ref(_layernorm(x, axis=-1), L0_ffn_gate_w, L0_ffn_gate_b, L0_ffn_w1, L0_ffn_b1, L0_ffn_w3, L0_ffn_b3, L0_ffn_w2, L0_ffn_b2, L0_ffn_sw1, L0_ffn_sb1, L0_ffn_sw3, L0_ffn_sb3, L0_ffn_sw2, L0_ffn_sb2)
    return x

_drawn_inputs = setup_inputs


def setup_inputs(seed=0):
    import zlib

    import numpy as np

    out = dict(_drawn_inputs(seed))
    spreads = {}
    factors = {'L0_xattn_b_q': 8.0,
     'L0_xattn_b_k': 64.0,
     'L0_xattn_b_v': 7.257,
     'L0_xattn_b_out': 7.279,
     'L0_ffn_gate_w': 8.0,
     'L0_ffn_gate_b': 8.0,
     'L0_ffn_w1': 8.0,
     'L0_ffn_b1': 8.0,
     'L0_ffn_w3': 8.0,
     'L0_ffn_b3': 8.0,
     'L0_ffn_w2': 8.0,
     'L0_ffn_b2': 28.711,
     'L0_ffn_sw1': 8.0,
     'L0_ffn_sb1': 8.0,
     'L0_ffn_sw3': 8.0,
     'L0_ffn_sb3': 8.0,
     'L0_ffn_sw2': 8.0,
     'L0_ffn_sb2': 16.755}
    for name, (base, spread) in spreads.items():
        noise = np.random.default_rng([zlib.crc32(name.encode()), seed]).standard_normal(out[name].shape)
        drawn = base * np.exp(spread * noise) if base else spread * noise
        out[name] = jnp.asarray(drawn.astype(out[name].dtype))
    for name, factor in factors.items():
        out[name] = (out[name] * factor).astype(out[name].dtype)
    return out
```

```python
from contextlib import ExitStack

import concourse.bass as bass
from concourse import mybir

F32 = mybir.dt.float32
F32R = mybir.dt.float32r
BF16 = mybir.dt.bfloat16
I32 = mybir.dt.int32
ALU = mybir.AluOpType
ACT = mybir.ActivationFunctionType
AX = mybir.AxisListType

P = 128
B = 16
D = 128
H = 16
DK = D // H
E = 8
HID = 176
ROWS = (E + 1) * HID
TILES = -(-ROWS // P)
BIAS_ROW = 64
CHUNK = 512
CHUNKS = B * P // CHUNK
G = 4
TERMS = 6 * DK
C_ROW = 96
PARTS = 3
RING = 4
WSLICE = TILES * P // B
LAG = 3
AHEAD = 8
EPS = 1e-5
MASKED = -(2.0 ** 60)
QSCALE = float(DK) ** -0.5
BF16_ONES = 1.0 + 0x3F80 / 2.0 ** 23


def build(nc, xc, mk, wqkvo, cols, rows, gate_w, ident, spread, experts, expert_cols, out):
    scratch = nc.dram_tensor("parts_scratch", (RING, 10 * DK, H * P), BF16, kind="Internal").ap()

    with ExitStack() as ctx:
        def sb(name, shape, dt=F32):
            return ctx.enter_context(nc.sbuf_tensor(name, shape, dt))

        def sem(name):
            return ctx.enter_context(nc.semaphore(name))

        def sems(name, n):
            return [sem(f"{name}{k}") for k in range(n)]

        bank = [ctx.enter_context(nc.psum_tensor(f"bank{k}", [P, 512], F32)) for k in range(8)]
        score_bank, prob_bank = bank[0:2], bank[2:4]
        value_bank, turn_bank, in_bank, out_bank = bank[4:8]
        z1_bank, z3_bank, spread_bank, y_bank, yt_bank = bank[0:2], bank[2:4], bank[4:6], bank[6], bank[7]

        w_sb = sb("w_sb", [P, 4 * D])
        cols_sb = sb("cols_sb", [P, 5])
        rows_sb = sb("rows_sb", [P, D + 2 * E])
        gate_sb = sb("gate_sb", [P, E])
        ident_sb = sb("ident_sb", [P, P])
        ident_bf = sb("ident_bf", [P, P], BF16)
        spread_sb = sb("spread_sb", [PARTS * (E + 1), TILES * P])
        spread_bf = sb("spread_bf", [P, TILES * P], BF16)
        we_in = sb("we_in", [P, 2, 3, WSLICE])
        we_hi = sb("we_hi", [P, 3, TILES * P], F32R)
        we_lo = sb("we_lo", [P, 3, TILES * P], F32R)
        ecols_sb = sb("ecols_sb", [P, 3, TILES])
        tanh_g = sb("tanh_g", [P, 2])
        bq_scaled = sb("bq_scaled", [P, 1])
        bo_gated = sb("bo_gated", [P, D])
        half = sb("half", [P, 1])
        xin = sb("xin", [P, RING, 2 * D])
        mask_in = sb("mask_in", [P, RING, 2 * P], I32)
        mask_add = sb("mask_add", [P, RING, 2 * P], BF16)
        stack = sb("stack", [P, RING, 2, H, P], BF16)
        v_one = sb("v_one", [P, RING, H, 32])
        x_bias = sb("x_bias", [P, RING, D])
        bn1 = sb("bn1", [P, 6])
        mv1 = sb("mv1", [P, 2, 2])
        var1 = sb("var1", [P, 1])
        rstd1 = sb("rstd1", [P, 2])
        shift1 = sb("shift1", [P, 2])
        xn = sb("xn", [P, 2, D])
        xn_t = sb("xn_t", [P, P])
        qk = sb("qk", [P, 2 * P])
        qk_rest = sb("qk_rest", [P, 2 * P])
        qk_parts = sb("qk_parts", [P, 2, 2 * PARTS, P], BF16)
        neg_max = sb("neg_max", [P, 2, H])
        max_rest = sb("max_rest", [P, H])
        max_parts = sb("max_parts", [P, PARTS * H], BF16)
        max_t = sb("max_t", [PARTS * H, 2, P], BF16)
        probs = sb("probs", [P, 4, G * P])
        values = sb("values", [P, G * P])
        recip = sb("recip", [P, H])
        attn = sb("attn", [P, D])
        attn_t = sb("attn_t", [P, P])
        x1 = sb("x1", [P, B, D])
        bn2 = sb("bn2", [P, 6])
        mv2 = sb("mv2", [P, 2])
        var2 = sb("var2", [P, 1])
        rstd2 = sb("rstd2", [P, 1])
        xn2 = sb("xn2", [P, D])
        xn2_t = sb("xn2_t", [P, P])
        x_hi = sb("x_hi", [P, B * P], F32R)
        x_lo = sb("x_lo", [P, B * P], F32R)
        logits = sb("logits", [P, B, E])
        r_max = sb("r_max", [P, B])
        r_sum = sb("r_sum", [P, B])
        r_a = sb("r_a", [P, B, E])
        r_score = sb("r_score", [P, B, E])
        r_bias = sb("r_bias", [P, B, E])
        r_pick = sb("r_pick", [P, B, E])
        r_sel = sb("r_sel", [P, 2, B, E])
        weight = sb("weight", [P, B, E + 1])
        weight_rest = sb("weight_rest", [P, B, E + 1])
        weight_parts = sb("weight_parts", [P, B, PARTS, E + 1], BF16)
        weight_t = sb("weight_t", [P, B * P], BF16)
        z3 = sb("z3", [P, 3, CHUNK])
        z = sb("z", [P, 3, CHUNK])
        act = sb("act", [P, 3, CHUNK])
        hid = sb("hid", [P, 3, CHUNK])
        hid_hi = sb("hid_hi", [P, 5, CHUNK], F32R)
        hid_lo = sb("hid_lo", [P, 5, CHUNK], F32R)
        y_t = sb("y_t", [P, CHUNK])

        s_const = sem("s_const")
        s_experts = sems("s_experts", 2)
        s_pad_q = sem("s_pad_q")
        s_pad_k = sem("s_pad_k")
        s_pad_v = sem("s_pad_v")
        s_half = sem("s_half")
        s_ident = sem("s_ident")
        s_tanh = sem("s_tanh")
        s_bq = sem("s_bq")
        s_bo = sem("s_bo")
        s_spread_in = sem("s_spread_in")
        s_spread_zero = sem("s_spread_zero")
        s_spread_bf = sem("s_spread_bf")
        s_loaded = sems("s_loaded", RING)
        s_bn1 = sem("s_bn1")
        s_stat1 = sem("s_stat1")
        s_var1 = sem("s_var1")
        s_rstd1 = sem("s_rstd1")
        s_shift1 = sem("s_shift1")
        s_xn = sem("s_xn")
        s_mask = sem("s_mask")
        s_xbias = sem("s_xbias")
        s_xn_t = sem("s_xn_t")
        s_xn_t_sb = sem("s_xn_t_sb")
        s_qkv = sem("s_qkv")
        s_qk_sb = sem("s_qk_sb")
        s_v_sb = sem("s_v_sb")
        s_part1 = sem("s_part1")
        s_rest1 = sem("s_rest1")
        s_part2 = sem("s_part2")
        s_parts = sem("s_parts")
        s_scratch = sems("s_scratch", 2)
        s_stack = sems("s_stack", RING)
        s_score = sem("s_score")
        s_max = sem("s_max")
        s_c1 = sem("s_c1")
        s_crest = sem("s_crest")
        s_c2 = sem("s_c2")
        s_c = sem("s_c")
        s_c_t = sem("s_c_t")
        s_c_t_sb = sem("s_c_t_sb")
        s_c_row = sems("s_c_row", RING)
        s_shifted = sem("s_shifted")
        s_exp = sem("s_exp")
        s_value = sem("s_value")
        s_value_sb = sem("s_value_sb")
        s_value_t = sem("s_value_t")
        s_recip = sem("s_recip")
        s_attn = sem("s_attn")
        s_attn_t = sem("s_attn_t")
        s_attn_t_sb = sem("s_attn_t_sb")
        s_proj = sem("s_proj")
        s_x1 = sem("s_x1")
        s_bn2 = sem("s_bn2")
        s_stat2 = sem("s_stat2")
        s_var2 = sem("s_var2")
        s_rstd2 = sem("s_rstd2")
        s_xn2 = sem("s_xn2")
        s_xn2_t = sem("s_xn2_t")
        s_xn2_t_sb = sem("s_xn2_t_sb")
        s_xhi = sem("s_xhi")
        s_xlo = sem("s_xlo")
        s_logit = sem("s_logit")
        s_logit_sb = sem("s_logit_sb")
        s_whi = sem("s_whi")
        s_wlo = sem("s_wlo")
        s_route = sem("s_route")
        s_route_exp = sem("s_route_exp")
        s_weight = sem("s_weight")
        s_weight_t = sem("s_weight_t")
        s_weight_sb = sem("s_weight_sb")
        s_z1 = sem("s_z1")
        s_z3 = sem("s_z3")
        s_spread = sem("s_spread")
        s_z3_sb = sem("s_z3_sb")
        s_z = sem("s_z")
        s_act = sem("s_act")
        s_hid = sem("s_hid")
        s_hid_hi = sem("s_hid_hi")
        s_hid_lo = sem("s_hid_lo")
        s_layer2 = sem("s_layer2")
        s_apart = sem("s_apart")
        s_y_sb = sem("s_y_sb")
        s_y_t = sem("s_y_t")
        s_result = sem("s_result")
        s_out = sem("s_out")

        N_CONST = 16 * 6

        def number(b):
            return 4 * b[0] + b[1]

        def place(b, n=RING):
            return b[1] % n

        def used(b, n=RING):
            return b[0] * (4 // n) + b[1] // n

        def after(b, n):
            return (b[0], b[1] + n)

        def exists(b):
            return not isinstance(b[0], int) or number(b) >= 0

        def need(eng, s, value):
            if not isinstance(value, int) or value > 0:
                eng.wait_ge(s, value)

        def apart(eng):
            eng.sem_inc(s_apart, 1)

        def in_bank_pair(m):
            return m % 2

        def twin(m):
            return m % 2 if m < TILES - 1 else 2

        def deep(m):
            return m % 4 if m < TILES - 1 else 4

        def before(c, m, where):
            back = next(d for d in range(1, 2 * TILES) if d == 5 or where((m - d) % TILES) == where(m))
            return TILES * c + m - back + 1

        def walk_tiles(eng, stage, late=None, lag=0, finish=None, finish_at=0):
            def step(c, m, c_before):
                if m < TILES:
                    stage(c, m)
                if late is not None and m - lag < TILES:
                    if m >= lag:
                        late(c, m - lag)
                    elif c_before is not None:
                        late(c_before, m - lag + TILES)
                if finish is not None:
                    if m == TILES + finish_at:
                        finish(c)
                    elif m == finish_at and c_before is not None:
                        finish(c_before)

            for m in range(AHEAD):
                step(0, m, None)
            with eng.Fori(0, CHUNKS - 1) as c:
                for m in range(AHEAD, TILES):
                    step(c, m, c)
                for m in range(AHEAD):
                    step(c + 1, m, c)
            for m in range(AHEAD, TILES + AHEAD):
                step(CHUNKS - 1, m, CHUNKS - 2)

        block = ctx.enter_context(nc.Block())

        @block.sync
        def _(sp):
            def load(b):
                need(sp, s_xbias, number(b) - RING + 1)
                need(sp, s_mask, number(b) - RING + 1)
                need(sp, s_qkv, number(b) - RING + 1)
                sp.dma_start(xin[:, place(b), :], xc[number(b)]).then_inc(s_loaded[place(b)], 16)
                sp.dma_start(mask_in[:, place(b), :], mk[number(b)]).then_inc(s_loaded[place(b)], 16)

            def store_parts(b):
                sp.wait_ge(s_parts, number(b) + 1)
                apart(sp)
                need(sp, s_stack[place(b)], 48 * used(b))
                sp.dma_start(scratch[place(b), 0:2 * PARTS * DK].rearrange("(n d) (h t) -> (d h) n t", d=DK, h=H),
                             qk_parts[:, place(b, 2)]).then_inc(s_scratch[place(b, 2)], 16)

            def fill_stacks(b):
                sp.wait_ge(s_scratch[place(b, 2)], 16 * used(b, 2) + 16)
                row = 0
                for n in (3, 2, 1):
                    apart_qk = (2 * PARTS - n) * DK
                    src = scratch[place(b), 0:2 * apart_qk].rearrange("(w r) x -> r w x", w=2)[0:n * DK]
                    sp.dma_start(stack[row:row + n * DK, place(b)].rearrange("r w h t -> r w (h t)"), src)\
                        .then_inc(s_stack[place(b)], 16)
                    row += n * DK

            def fill_max_rows(b):
                sp.wait_ge(s_c_t_sb, number(b) + 1)
                sp.dma_start(stack[C_ROW:C_ROW + PARTS, place(b), 0], max_t[:, place(b, 2), :])\
                    .then_inc(s_c_row[place(b)], 16)

            def load_weights(b):
                need(sp, s_wlo, number(b) - 1)
                apart(sp)
                c = bass.ds(number(b) * WSLICE, WSLICE)
                sp.dma_start(we_in[:, place(b, 2)], experts[:, :, c]).then_inc(s_experts[place(b, 2)], 16)

            def load_const(*pairs):
                for dst, src in pairs:
                    sp.dma_start(dst[:], src).then_inc(s_const, 16)

            load((0, 0))
            load_const((ident_sb, ident), (cols_sb, cols), (w_sb, wqkvo), (rows_sb, rows), (gate_sb, gate_w),
                       (ecols_sb, expert_cols))
            for j in range(1, RING):
                load((0, j))
            sp.dma_start(spread_sb[:], spread).then_inc(s_spread_in, 16)

            def padded(n):
                sp.wait_ge(s_pad_q, 2 * n)
                sp.wait_ge(s_pad_k, 3 * n)

            store_parts((0, 0))
            padded(1)
            fill_stacks((0, 0))
            store_parts((0, 1))
            padded(2)
            fill_stacks((0, 1))
            fill_max_rows((0, 0))
            store_parts((0, 2))
            load_weights((0, 0))
            padded(RING)

            def step(s, nxt=True, new=True, stack2=True, more=True):
                if more:
                    load(after(s, 4))
                if stack2:
                    fill_stacks(after(s, 2))
                if nxt:
                    fill_max_rows(after(s, 1))
                    load_weights(after(s, 1))
                if new:
                    store_parts(after(s, 3))

            with sp.Fori(0, 3) as i:
                for j in range(4):
                    step((i, j))
            step((3, 0), more=False)
            step((3, 1), more=False, new=False)
            step((3, 2), more=False, new=False, stack2=False)

            with sp.Fori(0, CHUNKS) as c:
                sp.wait_ge(s_result, c + 1)
                apart(sp)
                sp.dma_start(out.rearrange("(n p) d -> p n d", p=P)[:, bass.ds(4 * c, 4), :],
                             x1[:, bass.ds(4 * c, 4), :]).then_inc(s_out, 16)
            sp.wait_ge(s_out, 16 * CHUNKS)

        @block.gpsimd
        def _(pool):
            def pad_k(n):
                for m, (a, b, value) in enumerate(((32, 64, 0.0), (64, 96, 0.0), (96, 128, BF16_ONES))):
                    pool.memset(stack[a:b, n, 1].rearrange("p h t -> p (h t)").bitcast(F32), value).then_inc(s_pad_k, 1)
                    pool.wait_ge(s_pad_k, 3 * n + m + 1)

            pool.memset(half[:], -0.5).then_inc(s_half, 1)
            pool.wait_ge(s_half, 1)
            pad_k(0)

            def scale1(b):
                pool.wait_ge(s_stat1, number(b) + 1)
                apart(pool)
                pool.tensor_scalar(var1[:], mv1[:, place(b, 2), 1:2], EPS, None, ALU.add).then_inc(s_var1, 1)
                pool.wait_ge(s_var1, number(b) + 1)
                need(pool, s_xn, number(b) - 1)
                k = slice(place(b, 2), place(b, 2) + 1)
                apart(pool)
                pool.tensor_tensor(rstd1[:, k], var1[:], half[:], ALU.pow).then_inc(s_rstd1, 1)
                pool.wait_ge(s_rstd1, number(b) + 1)
                apart(pool)
                pool.tensor_scalar(shift1[:, k], mv1[:, place(b, 2), 0:1], rstd1[:, k], -1.0,
                                   ALU.mult, ALU.mult).then_inc(s_shift1, 1)

            def bias_x(b):
                need(pool, s_x1, number(b) - RING + 1)
                pool.tensor_tensor(x_bias[:, place(b), :], xin[:, place(b), 0:D], bo_gated[:], ALU.add)\
                    .then_inc(s_xbias, 1)

            def cut_max(b):
                pool.wait_ge(s_max, 4 * number(b) + 4)
                need(pool, s_c_t, number(b))
                m = neg_max[:, place(b, 2), :]
                apart(pool)
                pool.tensor_copy(max_parts[:, 0:H], m).then_inc(s_c1, 1)
                pool.wait_ge(s_c1, number(b) + 1)
                pool.tensor_tensor(max_rest[:], m, max_parts[:, 0:H], ALU.subtract).then_inc(s_crest, 1)
                pool.wait_ge(s_crest, number(b) + 1)
                apart(pool)
                pool.tensor_copy(max_parts[:, H:2 * H], max_rest[:]).then_inc(s_c2, 1)
                pool.wait_ge(s_c2, number(b) + 1)
                pool.tensor_tensor(max_parts[:, 2 * H:3 * H], max_rest[:], max_parts[:, H:2 * H], ALU.subtract)\
                    .then_inc(s_c, 1)

            def scale2(b):
                pool.wait_ge(s_stat2, number(b) + 1)
                need(pool, s_xn2, number(b))
                apart(pool)
                pool.tensor_scalar(var2[:], mv2[:, 1:2], EPS, None, ALU.add).then_inc(s_var2, 1)
                pool.wait_ge(s_var2, number(b) + 1)
                pool.tensor_tensor(rstd2[:], var2[:], half[:], ALU.pow).then_inc(s_rstd2, 1)

            def slice_of(b):
                return bass.ds(number(b) * WSLICE, WSLICE)

            def weights_hi(b):
                pool.wait_ge(s_experts[place(b, 2)], 16 * used(b, 2) + 16)
                apart(pool)
                pool.tensor_copy(we_hi[:, :, slice_of(b)], we_in[:, place(b, 2)]).then_inc(s_whi, 1)

            def weights_lo(b):
                pool.wait_ge(s_whi, number(b) + 1)
                pool.tensor_tensor(we_lo[:, :, slice_of(b)], we_in[:, place(b, 2)], we_hi[:, :, slice_of(b)],
                                   ALU.subtract).then_inc(s_wlo, 1)

            def x_lo_part(b):
                pool.wait_ge(s_xhi, number(b) + 1)
                c = bass.ds(number(b) * P, P)
                pool.tensor_tensor(x_lo[:, c], xn2_t[:], x_hi[:, c], ALU.subtract).then_inc(s_xlo, 1)

            scale1((0, 0))
            pool.wait_ge(s_const, N_CONST)
            pool.tensor_scalar(bq_scaled[:], cols_sb[:, 0:1], QSCALE, None, ALU.mult).then_inc(s_bq, 1)
            scale1((0, 1))
            pool.tensor_copy(ident_bf[:], ident_sb[:]).then_inc(s_ident, 1)
            pool.memset(v_one[:], 0.0).then_inc(s_pad_v, 1)
            pool.wait_ge(s_pad_v, 1)
            pool.memset(v_one[:, :, :, DK:DK + 1], 1.0).then_inc(s_pad_v, 1)
            pool.wait_ge(s_pad_v, 2)
            pad_k(1)
            scale1((0, 2))
            pool.wait_ge(s_shift1, 3)
            pad_k(2)
            cut_max((0, 0))
            pool.wait_ge(s_tanh, 1)
            pool.tensor_scalar(bo_gated[:], rows_sb[:, 0:D], tanh_g[:, 0:1], None, ALU.mult).then_inc(s_bo, 1)
            pool.wait_ge(s_bo, 1)
            for j in range(3):
                bias_x((0, j))
            pool.wait_ge(s_xbias, 3)
            pad_k(3)

            def step(s, prev=True, nxt=True, new=True):
                if new:
                    scale1(after(s, 3))
                weights_hi(s)
                if nxt:
                    cut_max(after(s, 1))
                if prev:
                    scale2(after(s, -1))
                if new:
                    bias_x(after(s, 3))
                weights_lo(s)
                if prev:
                    x_lo_part(after(s, -1))

            step((0, 0), prev=False)
            with pool.Fori(0, 3) as i:
                for j in range(1, 5):
                    step((i, j))
            step((3, 1), new=False)
            step((3, 2), new=False)
            step((3, 3), new=False, nxt=False)
            scale2((3, 3))
            x_lo_part((3, 3))
            pool.wait_ge(s_spread_in, 16)
            pool.wait_ge(s_spread_zero, 2)
            pool.tensor_copy(spread_bf[0:PARTS * (E + 1), :], spread_sb[:]).then_inc(s_spread_bf, 1)

            def cut_hidden(c, m):
                n = TILES * c + m
                pool.wait_ge(s_hid_hi, n + 1)
                need(pool, s_layer2, before(c, m, deep))
                pool.tensor_tensor(hid_lo[:, deep(m)], hid[:, twin(m)], hid_hi[:, deep(m)], ALU.subtract)\
                    .then_inc(s_hid_lo, 1)

            walk_tiles(pool, cut_hidden)

        @block.scalar
        def _(act_e):
            act_e.wait_ge(s_const, N_CONST)
            act_e.activation(tanh_g[:], cols_sb[:, 3:5], ACT.Tanh).then_inc(s_tanh, 1)

            def normalise(b):
                act_e.wait_ge(s_shift1, number(b) + 1)
                need(act_e, s_xn_t, number(b) - 1)
                k = slice(place(b, 2), place(b, 2) + 1)
                act_e.activation(xn[:, place(b, 2), :], xin[:, place(b), 0:D], ACT.Identity, bias=shift1[:, k],
                                 scale=rstd1[:, k]).then_inc(s_xn, 1)

            def copy_xn_t(b):
                act_e.wait_ge(s_xn_t, number(b) + 1)
                need(act_e, s_qkv, number(b))
                act_e.activation(xn_t[:], in_bank[:, 384:512], ACT.Copy).then_inc(s_xn_t_sb, 1)

            def copy_qk(b):
                act_e.wait_ge(s_qkv, number(b) + 1)
                need(act_e, s_rest1, number(b))
                act_e.activation(qk[:, 0:P], in_bank[:, 0:P], ACT.Identity, bias=bq_scaled[:, 0:1],
                                 scale=QSCALE).then_inc(s_qk_sb, 1)
                act_e.activation(qk[:, P:2 * P], in_bank[:, P:2 * P], ACT.Identity, bias=cols_sb[:, 1:2])\
                    .then_inc(s_qk_sb, 1)

            def copy_v(b):
                need(act_e, s_value, 4 * number(b) - 4 * (RING - 1))
                act_e.activation(v_one[:, place(b), :, 0:DK],
                                 in_bank[:, 256:384].rearrange("p (h d) -> p h d", d=DK), ACT.Copy)\
                    .then_inc(s_v_sb, 1)

            def copy_max_t(b):
                act_e.wait_ge(s_c_t, number(b) + 1)
                o = after(b, -2)
                if exists(o):
                    act_e.wait_ge(s_c_row[place(o)], 16 * used(o) + 16)
                act_e.activation(max_t[:, place(b, 2), :], turn_bank[0:PARTS * H, 0:P // 2].bitcast(BF16), ACT.Copy)\
                    .then_inc(s_c_t_sb, 1)

            def exp(b, g):
                act_e.wait_ge(s_shifted, 4 * number(b) + g + 1)
                need(act_e, s_value, 4 * number(b) + g - 3)
                act_e.activation(probs[:, g, :], prob_bank[g % 2][:, :], ACT.Exp).then_inc(s_exp, 1)

            def copy_values(b):
                act_e.wait_ge(s_value, 4 * number(b) + 4)
                need(act_e, s_value_t, number(b))
                act_e.activation(values[:], value_bank[:, :], ACT.Copy).then_inc(s_value_sb, 1)

            def copy_attn_t(b):
                act_e.wait_ge(s_attn_t, number(b) + 1)
                need(act_e, s_proj, number(b))
                act_e.activation(attn_t[:], out_bank[:, 0:P], ACT.Identity, bias=cols_sb[:, 2:3])\
                    .then_inc(s_attn_t_sb, 1)

            def copy_xn2_t(b):
                act_e.wait_ge(s_xn2_t, number(b) + 1)
                need(act_e, s_logit, number(b))
                need(act_e, s_xlo, number(b))
                act_e.activation(xn2_t[:], out_bank[:, 0:P], ACT.Copy).then_inc(s_xn2_t_sb, 1)
                act_e.activation(x_hi[:, bass.ds(number(b) * P, P)], out_bank[:, 0:P], ACT.Copy).then_inc(s_xhi, 1)

            def copy_logits(b):
                act_e.wait_ge(s_logit, number(b) + 1)
                act_e.activation(logits[:, bass.ds(number(b), 1), :].rearrange("p n e -> p (n e)"),
                                 out_bank[:, 0:E], ACT.Copy).then_inc(s_logit_sb, 1)

            normalise((0, 0))
            act_e.wait_ge(s_bq, 1)
            for j in range(3):
                copy_xn_t((0, j))
                copy_qk((0, j))
                if j < 2:
                    normalise((0, j + 1))
                act_e.wait_ge(s_pad_v, 2)
                copy_v((0, j))
            copy_max_t((0, 0))

            def step(s, prev=True, nxt=True, new=True):
                if prev:
                    copy_values(after(s, -1))
                if new:
                    normalise(after(s, 3))
                    copy_xn_t(after(s, 3))
                if prev:
                    copy_attn_t(after(s, -1))
                exp(s, 0)
                exp(s, 1)
                if new:
                    copy_qk(after(s, 3))
                    copy_v(after(s, 3))
                exp(s, 2)
                if nxt:
                    copy_max_t(after(s, 1))
                exp(s, 3)
                if prev:
                    copy_xn2_t(after(s, -1))
                    copy_logits(after(s, -1))

            step((0, 0), prev=False)
            with act_e.Fori(0, 3) as i:
                for j in range(1, 5):
                    step((i, j))
            step((3, 1), new=False)
            step((3, 2), new=False)
            step((3, 3), new=False, nxt=False)
            copy_values((3, 3))
            copy_attn_t((3, 3))
            copy_xn2_t((3, 3))
            copy_logits((3, 3))

            act_e.wait_ge(s_route, 2)
            act_e.activation(r_a[:], r_a[:], ACT.Exp).then_inc(s_route_exp, 1)
            for n in range(2):
                act_e.wait_ge(s_weight_t, n + 1)
                act_e.activation(weight_t[0:PARTS * (E + 1), n * 1024:(n + 1) * 1024],
                                 yt_bank[0:PARTS * (E + 1), :].bitcast(BF16), ACT.Copy).then_inc(s_weight_sb, 1)

            def copy_z3(c, m):
                act_e.wait_ge(s_z3, TILES * c + m + 1)
                need(act_e, s_z, before(c, m, twin))
                act_e.activation(z3[:, twin(m)], z3_bank[in_bank_pair(m)][:, :], ACT.Identity,
                                 bias=ecols_sb[:, 1, m:m + 1]).then_inc(s_z3_sb, 1)

            def silu(c, m):
                act_e.wait_ge(s_z, TILES * c + m + 1)
                need(act_e, s_hid, before(c, m, twin))
                act_e.activation(act[:, twin(m)], z[:, twin(m)], ACT.Silu).then_inc(s_act, 1)

            def copy_y(c):
                act_e.wait_ge(s_layer2, TILES * c + TILES)
                act_e.activation(y_t[:], y_bank[:, :], ACT.Copy, scale=tanh_g[:, 1:2]).then_inc(s_y_sb, 1)

            walk_tiles(act_e, copy_z3, silu, 1, copy_y, LAG)

        @block.vector
        def _(dve):
            def stats1(b):
                dve.wait_ge(s_loaded[place(b)], 32 * used(b) + 32)
                need(dve, s_stat1, number(b))
                dve.bn_stats(bn1[:], xin[:, place(b), 0:D]).then_inc(s_bn1, 1)
                dve.wait_ge(s_bn1, number(b) + 1)
                need(dve, s_shift1, number(b) - 1)
                apart(dve)
                dve.bn_aggr(mv1[:, place(b, 2), :], bn1[:]).then_inc(s_stat1, 1)

            def add_of_mask(b):
                dve.wait_ge(s_loaded[place(b)], 32 * used(b) + 32)
                need(dve, s_shifted, 4 * number(b) - 4 * (RING - 1))
                apart(dve)
                dve.tensor_scalar(mask_add[:, place(b), :], mask_in[:, place(b), :], 0.0, MASKED,
                                  ALU.is_equal, ALU.mult).then_inc(s_mask, 1)

            def part(b, i):
                return qk_parts[:, place(b, 2), i:2 * PARTS - i:2 * PARTS - 1 - 2 * i]

            qk_pair = qk[:].rearrange("p (w t) -> p w t", w=2)
            rest_pair = qk_rest[:].rearrange("p (w t) -> p w t", w=2)

            def cut1(b):
                dve.wait_ge(s_qk_sb, 2 * number(b) + 2)
                need(dve, s_scratch[place(b, 2)], 16 * used(b, 2))
                dve.tensor_copy(part(b, 0), qk_pair).then_inc(s_part1, 1)

            def cut2(b):
                dve.wait_ge(s_part1, number(b) + 1)
                dve.tensor_tensor(rest_pair, qk_pair, part(b, 0), ALU.subtract).then_inc(s_rest1, 1)

            def cut3(b):
                dve.wait_ge(s_rest1, number(b) + 1)
                dve.tensor_copy(part(b, 1), rest_pair).then_inc(s_part2, 1)

            def cut4(b):
                dve.wait_ge(s_part2, number(b) + 1)
                dve.tensor_tensor(part(b, 2), rest_pair, part(b, 1), ALU.subtract).then_inc(s_parts, 1)

            def cut_qk(b):
                for cut in (cut1, cut2, cut3, cut4):
                    cut(b)

            def row_max(b, g):
                dve.wait_ge(s_score, 4 * number(b) + g + 1)
                if g == 0:
                    need(dve, s_c, number(b) - 1)
                dve.tensor_reduce(neg_max[:, place(b, 2), G * g:G * g + G],
                                  score_bank[g % 2][:, :].rearrange("p (h k) -> p h k", h=G), AX.X, ALU.max,
                                  negate=True).then_inc(s_max, 1)

            def divide(b):
                dve.wait_ge(s_value_t, number(b) + 1)
                t = turn_bank[:, :].rearrange("p (h c) -> p h c", c=32)
                dve.reciprocal(recip[:].rearrange("p (h c) -> p h c", c=1), t[:, :, DK:DK + 1]).then_inc(s_recip, 1)
                dve.wait_ge(s_recip, number(b) + 1)
                need(dve, s_attn_t, number(b))
                dve.tensor_tensor(attn[:].rearrange("p (h d) -> p h d", d=DK), t[:, :, 0:DK],
                                  recip[:].rearrange("p (h c) -> p h c", c=1).broadcast_to([P, H, DK]),
                                  ALU.mult).then_inc(s_attn, 1)

            def residual(b):
                dve.wait_ge(s_proj, number(b) + 1)
                dve.wait_ge(s_xbias, number(b) + 1)
                x1_b = x1[:, bass.ds(number(b), 1), :].rearrange("p n d -> p (n d)")
                dve.scalar_tensor_tensor(x1_b, out_bank[:, 0:D], tanh_g[:, 0:1], x_bias[:, place(b), :],
                                         ALU.mult, ALU.add).then_inc(s_x1, 1)
                dve.wait_ge(s_x1, number(b) + 1)
                apart(dve)
                dve.bn_stats(bn2[:], x1_b).then_inc(s_bn2, 1)

            def stats2(b):
                dve.wait_ge(s_bn2, number(b) + 1)
                need(dve, s_xn2, number(b))
                apart(dve)
                dve.bn_aggr(mv2[:], bn2[:]).then_inc(s_stat2, 1)

            def normalise2(b):
                dve.wait_ge(s_rstd2, number(b) + 1)
                need(dve, s_xn2_t, number(b))
                dve.tensor_scalar(xn2[:], x1[:, bass.ds(number(b), 1), :].rearrange("p n d -> p (n d)"),
                                  mv2[:, 0:1], rstd2[:], ALU.subtract, ALU.mult).then_inc(s_xn2, 1)

            def pad_q(n):
                for a, b in ((32, 64), (64, 128)):
                    dve.memset(stack[a:b, n, 0].rearrange("p h t -> p (h t)").bitcast(F32), 0.0).then_inc(s_pad_q, 1)

            pad_q(0)
            stats1((0, 0))
            add_of_mask((0, 0))
            stats1((0, 1))
            cut_qk((0, 0))
            pad_q(1)
            stats1((0, 2))
            add_of_mask((0, 1))
            cut_qk((0, 1))
            pad_q(2)
            add_of_mask((0, 2))
            cut_qk((0, 2))
            for g in range(4):
                row_max((0, 0), g)
            pad_q(3)
            dve.memset(weight_t[:], 0.0).then_inc(s_spread_zero, 1)
            dve.memset(spread_bf[:], 0.0).then_inc(s_spread_zero, 1)

            def step(s, prev=True, nxt=True, new=True):
                p, n, w = after(s, -1), after(s, 1), after(s, 3)
                if new:
                    stats1(w)
                if nxt:
                    row_max(n, 0)
                    row_max(n, 1)
                if prev:
                    divide(p)
                if nxt:
                    row_max(n, 2)
                    row_max(n, 3)
                if new:
                    add_of_mask(w)
                if prev:
                    residual(p)
                    stats2(p)
                if new:
                    cut1(w)
                    cut2(w)
                if prev:
                    normalise2(p)
                if new:
                    cut3(w)
                    cut4(w)

            dve.wait_ge(s_tanh, 1)
            step((0, 0), prev=False)
            with dve.Fori(0, 3) as i:
                for j in range(1, 5):
                    step((i, j))
            step((3, 1), new=False)
            step((3, 2), new=False)
            step((3, 3), new=False, nxt=False)
            divide((3, 3))
            residual((3, 3))
            stats2((3, 3))
            normalise2((3, 3))

            chain = 0

            def col(t):
                return t[:].rearrange("p (n c) -> p n c", c=1).broadcast_to([P, B, E])

            def row(t):
                return t.rearrange("p (n e) -> p n e", n=1).broadcast_to([P, B, E])

            def then(ins):
                nonlocal chain
                chain += 1
                ins.then_inc(s_route, 1)
                dve.wait_ge(s_route, chain)

            dve.wait_ge(s_logit_sb, B)
            then(dve.tensor_reduce(r_max[:], logits[:], AX.X, ALU.max))
            then(dve.tensor_tensor(r_a[:], logits[:], col(r_max), ALU.subtract))
            dve.wait_ge(s_route_exp, 1)
            then(dve.tensor_reduce(r_sum[:], r_a[:], AX.X, ALU.add))
            then(dve.reciprocal(r_sum[:], r_sum[:]))
            then(dve.tensor_tensor(r_score[:], r_a[:], col(r_sum), ALU.mult))
            then(dve.tensor_tensor(r_bias[:], r_score[:], row(rows_sb[:, D:D + E]), ALU.add))
            for k in range(2):
                then(dve.tensor_reduce(r_max[:], r_bias[:], AX.X, ALU.max))
                then(dve.tensor_tensor(r_pick[:], r_bias[:], col(r_max), ALU.is_equal))
                then(dve.tensor_tensor(r_pick[:], r_pick[:], row(rows_sb[:, D + E:D + 2 * E]), ALU.mult))
                then(dve.tensor_reduce(r_max[:], r_pick[:], AX.X, ALU.max))
                then(dve.tensor_tensor(r_sel[:, k], r_pick[:], col(r_max), ALU.is_equal))
                if k == 0:
                    then(dve.scalar_tensor_tensor(r_bias[:], r_sel[:, 0], -3e38, r_bias[:], ALU.mult, ALU.add))
            then(dve.tensor_tensor(r_pick[:], r_sel[:, 0], r_sel[:, 1], ALU.add))
            then(dve.memset(weight[:, :, E:E + 1], 1.0))
            then(dve.tensor_tensor(weight[:, :, 0:E], r_score[:], r_pick[:], ALU.mult))
            then(dve.tensor_copy(weight_parts[:, :, 0], weight[:]))
            then(dve.tensor_tensor(weight_rest[:], weight[:], weight_parts[:, :, 0], ALU.subtract))
            then(dve.tensor_copy(weight_parts[:, :, 1], weight_rest[:]))
            dve.tensor_tensor(weight_parts[:, :, 2], weight_rest[:], weight_parts[:, :, 1], ALU.subtract)\
                .then_inc(s_weight, 1)

            def gate(c, m):
                n = TILES * c + m
                dve.wait_ge(s_z1, n + 1)
                dve.wait_ge(s_z3_sb, n + 1)
                need(dve, s_act, before(c, m, twin))
                dve.scalar_tensor_tensor(z[:, twin(m)], z1_bank[in_bank_pair(m)][:, :], ecols_sb[:, 0, m:m + 1],
                                         z3[:, twin(m)], ALU.add, ALU.mult).then_inc(s_z, 1)

            def weigh(c, m):
                n = TILES * c + m
                dve.wait_ge(s_act, n + 1)
                dve.wait_ge(s_spread, n + 1)
                need(dve, s_hid_lo, before(c, m, twin))
                dve.scalar_tensor_tensor(hid[:, twin(m)], act[:, twin(m)], ecols_sb[:, 2, m:m + 1],
                                         spread_bank[in_bank_pair(m)][:, :], ALU.add, ALU.mult).then_inc(s_hid, 1)
                dve.wait_ge(s_hid, n + 1)
                need(dve, s_layer2, before(c, m, deep))
                dve.tensor_copy(hid_hi[:, deep(m)], hid[:, twin(m)]).then_inc(s_hid_hi, 1)

            def finish(c):
                dve.wait_ge(s_y_t, c + 1)
                x1_c = x1[:, bass.ds(4 * c, 4), :].rearrange("p n d -> p (n d)")
                dve.tensor_tensor(x1_c, yt_bank[:, :], x1_c, ALU.add).then_inc(s_result, 1)

            walk_tiles(dve, gate, weigh, 1, finish, LAG + 2)

        @block.tensor
        def _(pe):
            def turn_xn(b):
                pe.wait_ge(s_xn, number(b) + 1)
                need(pe, s_v_sb, number(b))
                pe.transpose(in_bank[:, 384:512], xn[:, place(b, 2), :], ident_sb[:]).then_inc(s_xn_t, 1)

            def project_in(b):
                pe.wait_ge(s_xn_t_sb, number(b) + 1)
                ctx_t = xin[:, place(b), D:2 * D]
                pe.matmul(in_bank[:, 0:P], w_sb[:, 0:D], xn_t[:], start=True, stop=True)
                pe.matmul(in_bank[:, P:2 * P], w_sb[:, D:2 * D], ctx_t, start=True, stop=True)
                pe.matmul(in_bank[:, 2 * P:3 * P], ctx_t, w_sb[:, 2 * D:3 * D], start=True, stop=True)\
                    .then_inc(s_qkv, 1)

            def scores(b, g):
                if g == 0:
                    pe.wait_ge(s_stack[place(b)], 48 * used(b) + 48)
                    pe.wait_ge(s_mask, number(b) + 1)
                need(pe, s_max, 4 * number(b) + g - 1)
                o = score_bank[g % 2]
                for n in range(G):
                    pe.matmul(o[:, n * P:(n + 1) * P], stack[0:C_ROW, place(b), 0, G * g + n, :],
                              stack[0:C_ROW, place(b), 1, G * g + n, :], start=n == 0, stop=False,
                              skip_group_check=True)
                pe.matmul(o[:, :].rearrange("p (n k) -> p n k", n=G), ident_bf[:],
                          mask_add[:, place(b), 0:P].rearrange("p (n k) -> p n k", n=1).broadcast_to([P, G, P]),
                          start=False, stop=True, skip_group_check=True).then_inc(s_score, 1)

            def shifted(b, g):
                if g == 0:
                    pe.wait_ge(s_c_row[place(b)], 16 * used(b) + 16)
                need(pe, s_exp, 4 * number(b) + g - 1)
                o = prob_bank[g % 2]
                for n in range(G):
                    pe.matmul(o[:, n * P:(n + 1) * P], stack[:, place(b), 1, G * g + n, :],
                              stack[:, place(b), 0, G * g + n, :], start=n == 0, stop=False,
                              skip_group_check=True)
                pe.matmul(o[:, :].rearrange("p (n k) -> p n k", n=G), ident_bf[:],
                          mask_add[:, place(b), P:2 * P].rearrange("p (n k) -> p n k", n=1).broadcast_to([P, G, P]),
                          start=False, stop=True, skip_group_check=True).then_inc(s_shifted, 1)

            def weigh_values(b, g):
                pe.wait_ge(s_exp, 4 * number(b) + g + 1)
                if g == 0:
                    pe.wait_ge(s_v_sb, number(b) + 1)
                    need(pe, s_value_sb, number(b))
                for n in range(G):
                    mm = pe.matmul(value_bank[32 * n:32 * n + 32, g * P:(g + 1) * P], v_one[:, place(b), G * g + n, :],
                                   probs[:, g, n * P:(n + 1) * P], start=True, stop=True)
                mm.then_inc(s_value, 1)

            def turn_values(b):
                pe.wait_ge(s_value_sb, number(b) + 1)
                pe.wait_ge(s_c_t_sb, number(b) + 2 if not isinstance(b[0], int) else min(number(b) + 2, B))
                for g in range(4):
                    t = pe.transpose(turn_bank[:, g * P:(g + 1) * P], values[:, g * P:(g + 1) * P], ident_sb[:])
                t.then_inc(s_value_t, 1)

            def turn_attn(b):
                pe.wait_ge(s_attn, number(b) + 1)
                need(pe, s_logit_sb, number(b))
                pe.transpose(out_bank[:, 0:P], attn[:], ident_sb[:]).then_inc(s_attn_t, 1)

            def project_out(b):
                pe.wait_ge(s_attn_t_sb, number(b) + 1)
                pe.matmul(out_bank[:, 0:P], attn_t[:], w_sb[:, 3 * D:4 * D], start=True, stop=True)\
                    .then_inc(s_proj, 1)

            def turn_max(b):
                pe.wait_ge(s_c, number(b) + 1)
                need(pe, s_attn, number(b) - 1)
                apart(pe)
                pe.transpose(turn_bank[0:PARTS * H, 0:P // 2].bitcast(BF16), max_parts[:], ident_bf[:]).then_inc(s_c_t, 1)

            def turn_xn2(b):
                pe.wait_ge(s_xn2, number(b) + 1)
                pe.transpose(out_bank[:, 0:P], xn2[:], ident_sb[:]).then_inc(s_xn2_t, 1)

            def route(b):
                pe.wait_ge(s_xhi, number(b) + 1)
                pe.matmul(out_bank[:, 0:E], xn2_t[:], gate_sb[:], start=True, stop=True).then_inc(s_logit, 1)

            pe.wait_ge(s_const, N_CONST)
            for j in range(3):
                turn_xn((0, j))
                project_in((0, j))
            pe.wait_ge(s_ident, 1)
            for g in range(4):
                scores((0, 0), g)
            turn_max((0, 0))

            def step(s, prev=True, nxt=True, new=True):
                p, n, w = after(s, -1), after(s, 1), after(s, 3)
                if nxt:
                    scores(n, 0)
                    scores(n, 1)
                if prev:
                    turn_values(p)
                if nxt:
                    scores(n, 2)
                    scores(n, 3)
                if new:
                    turn_xn(w)
                if prev:
                    turn_attn(p)
                shifted(s, 0)
                shifted(s, 1)
                if prev:
                    project_out(p)
                if new:
                    project_in(w)
                weigh_values(s, 0)
                shifted(s, 2)
                if nxt:
                    turn_max(n)
                weigh_values(s, 1)
                shifted(s, 3)
                weigh_values(s, 2)
                if prev:
                    turn_xn2(p)
                weigh_values(s, 3)
                if prev:
                    route(p)

            step((0, 0), prev=False)
            with pe.Fori(0, 3) as i:
                for j in range(1, 5):
                    step((i, j))
            step((3, 1), new=False)
            step((3, 2), new=False)
            step((3, 3), new=False, nxt=False)
            turn_values((3, 3))
            turn_attn((3, 3))
            project_out((3, 3))
            turn_xn2((3, 3))
            route((3, 3))

            pe.wait_ge(s_weight, 1)
            pe.wait_ge(s_x1, B)
            for n in range(2):
                need(pe, s_weight_sb, n)
                for t in range(8):
                    tr = pe.transpose(yt_bank[0:PARTS * (E + 1), 64 * t:64 * t + 64].bitcast(BF16),
                                      weight_parts[:, 8 * n + t].rearrange("p i e -> p (i e)"), ident_bf[:])
                tr.then_inc(s_weight_t, 1)
            pe.wait_ge(s_weight_sb, 2)
            pe.wait_ge(s_spread_bf, 1)
            pe.wait_ge(s_wlo, B)
            pe.wait_ge(s_xlo, B)
            pe.wait_ge(s_max, 4 * B)
            pe.wait_ge(s_exp, 4 * B)
            pe.wait_ge(s_logit_sb, B)
            pe.wait_ge(s_v_sb, B)

            def layer1(c, m):
                cols_m = slice(m * P, (m + 1) * P)
                tok = bass.ds(c * CHUNK, CHUNK)
                k = in_bank_pair(m)
                for w, o, done, read in ((1, z3_bank[k], s_z3, s_z3_sb), (0, z1_bank[k], s_z1, s_z)):
                    need(pe, read, before(c, m, in_bank_pair))
                    pe.matmul(o[:, :], we_hi[:, w, cols_m], x_hi[:, tok], start=True, stop=False)
                    pe.matmul(o[:, :], we_hi[:, w, cols_m], x_lo[:, tok], start=False, stop=False)
                    pe.matmul(o[:, :], we_lo[:, w, cols_m], x_hi[:, tok], start=False, stop=True).then_inc(done, 1)
                need(pe, s_hid, before(c, m, in_bank_pair))
                pe.matmul(spread_bank[k][:, :], spread_bf[:, cols_m], weight_t[:, tok],
                          start=True, stop=True).then_inc(s_spread, 1)

            def layer2(c, m):
                n = TILES * c + m
                cols_m = slice(m * P, (m + 1) * P)
                pe.wait_ge(s_hid_lo, n + 1)
                if m == 0:
                    need(pe, s_y_sb, c)
                pe.matmul(y_bank[:, :], we_hi[:, 2, cols_m], hid_hi[:, deep(m)], start=m == 0, stop=False)
                pe.matmul(y_bank[:, :], we_lo[:, 2, cols_m], hid_hi[:, deep(m)], start=False, stop=False)
                pe.matmul(y_bank[:, :], we_hi[:, 2, cols_m], hid_lo[:, deep(m)], start=False, stop=m == TILES - 1)\
                    .then_inc(s_layer2, 1)

            def turn_y(c):
                pe.wait_ge(s_y_sb, c + 1)
                for t in range(CHUNK // P):
                    tr = pe.transpose(yt_bank[:, t * P:(t + 1) * P], y_t[:, t * P:(t + 1) * P], ident_sb[:])
                tr.then_inc(s_y_t, 1)

            walk_tiles(pe, layer1, layer2, LAG, turn_y, LAG + 1)


def kernel(**inputs):
    import numpy as np
    import concourse.bacc as bacc
    from concourse.bass_utils import run_bass_kernel_spmd

    f = {name: np.asarray(a) for name, a in inputs.items()}
    x, ctx, mask = f["x"], f["ctx_1024"], f["mask_Bx1xSxS2_ik0"][:, 0]
    by_d = np.arange(H * DK).reshape(H, DK).T.reshape(-1)
    wq, bq = f["L0_xattn_w_q"][by_d], f["L0_xattn_b_q"][by_d]
    wk, bk = f["L0_xattn_w_k"][by_d], f["L0_xattn_b_k"][by_d]

    def all_rows(routed, shared, first):
        a = np.concatenate([routed, shared[None]], 0)
        a = np.moveaxis(a, 0, first).reshape(*([D] if first else []), ROWS)
        return np.pad(a, [(0, 0)] * (a.ndim - 1) + [(0, TILES * P - ROWS)])

    w1 = all_rows(f["L0_ffn_w1"], f["L0_ffn_sw1"], 1)
    w3 = all_rows(f["L0_ffn_w3"], f["L0_ffn_sw3"], 1)
    w2 = np.zeros((TILES * P, D), np.float32)
    w2[:ROWS] = np.concatenate([f["L0_ffn_w2"].reshape(-1, D), f["L0_ffn_sw2"]])
    bias = (TILES - 1) * P + BIAS_ROW
    w2[bias:bias + E + 1] = np.concatenate([f["L0_ffn_b2"], f["L0_ffn_sb2"][None]])
    w2 = w2.reshape(TILES, P, D).transpose(1, 0, 2).reshape(P, TILES * D)
    is_bias = np.zeros(TILES * P, np.float32)
    is_bias[bias:bias + E + 1] = 1
    ecols = np.stack([all_rows(f["L0_ffn_b1"], f["L0_ffn_sb1"], 0), all_rows(f["L0_ffn_b3"], f["L0_ffn_sb3"], 0),
                      is_bias])
    spread = np.zeros((E + 1, TILES * P), np.float32)
    for e in range(E + 1):
        spread[e, e * HID:(e + 1) * HID] = 1
        spread[e, bias + e] = 1

    def everywhere(*rows):
        return np.broadcast_to(np.concatenate(rows)[None], (P, sum(map(len, rows))))

    arrays = {
        "xc": np.concatenate([x, ctx.transpose(0, 2, 1)], 2),
        "mk": np.concatenate([mask, mask.transpose(0, 2, 1)], 2),
        "wqkvo": np.concatenate([wq.T, wk.T, f["L0_xattn_w_v"].T, f["L0_xattn_w_out"].T], 1),
        "cols": np.concatenate([np.stack([bq, bk, f["L0_xattn_b_v"]], 1), everywhere(f["g_xattn"], f["g_ffn"])], 1),
        "rows": everywhere(f["L0_xattn_b_out"], f["L0_ffn_gate_b"], np.arange(E, 0, -1, dtype=np.float32)),
        "gate_w": f["L0_ffn_gate_w"].T,
        "ident": np.eye(P, dtype=np.float32),
        "spread": np.concatenate([spread] * PARTS),
        "experts": np.stack([w1, w3, w2], 1),
        "expert_cols": ecols.reshape(3, TILES, P).transpose(2, 0, 1),
    }
    arrays = {name: np.ascontiguousarray(a) for name, a in arrays.items()}
    nc = bacc.Bacc("TRN2", target_bir_lowering=False, num_devices=1)
    aps = {name: nc.dram_tensor(name, a.shape, mybir.dt.from_np(a.dtype), kind="ExternalInput").ap()
           for name, a in arrays.items()}
    out = nc.dram_tensor("out", (B * P, D), F32, kind="ExternalOutput").ap()
    build(nc, out=out, **aps)
    r = run_bass_kernel_spmd(nc, [arrays], core_ids=[0])
    return r.results[0]["out"].reshape(B, P, D)
```

```python
from contextlib import ExitStack

import concourse.bass as bass
from concourse import mybir

F32 = mybir.dt.float32
F32R = mybir.dt.float32r
BF16 = mybir.dt.bfloat16
I32 = mybir.dt.int32
ALU = mybir.AluOpType
ACT = mybir.ActivationFunctionType
AX = mybir.AxisListType

P = 128
B = 16
D = 128
H = 16
DK = D // H
E = 8
HID = 176
ROWS = (E + 1) * HID
TILES = -(-ROWS // P)
BIAS_ROW = 64
CHUNK = 512
CHUNKS = B * P // CHUNK
G = 4
TERMS = 6 * DK
C_ROW = 96
PARTS = 3
RING = 4
WSLICE = TILES * P // B
LAG = 3
EARLY = 12
EPS = 1e-5
MASKED = -(2.0 ** 60)
QSCALE = float(DK) ** -0.5
BF16_ONES = 1.0 + 0x3F80 / 2.0 ** 23


def build(nc, xc, mk, wqkvo, cols, rows, gate_w, ident, spread, experts, expert_cols, out):
    scratch = nc.dram_tensor("parts_scratch", (RING, 10 * DK, H * P), BF16, kind="Internal").ap()

    with ExitStack() as ctx:
        def sb(name, shape, dt=F32):
            return ctx.enter_context(nc.sbuf_tensor(name, shape, dt))

        def sem(name):
            return ctx.enter_context(nc.semaphore(name))

        def sems(name, n):
            return [sem(f"{name}{k}") for k in range(n)]

        bank = [ctx.enter_context(nc.psum_tensor(f"bank{k}", [P, 512], F32)) for k in range(8)]
        score_bank, prob_bank = bank[0:2], bank[2:4]
        value_bank, turn_bank, in_bank, out_bank = bank[4:8]
        z1_bank, z3_bank, spread_bank, y_bank, yt_bank = bank[0:2], bank[2:4], [in_bank, value_bank], bank[5], bank[7]

        w_sb = sb("w_sb", [P, 4 * D])
        cols_sb = sb("cols_sb", [P, 5])
        rows_sb = sb("rows_sb", [P, D + 2 * E])
        gate_sb = sb("gate_sb", [P, E])
        ident_sb = sb("ident_sb", [P, P])
        ident_bf = sb("ident_bf", [P, P], BF16)
        spread_sb = sb("spread_sb", [P, TILES * P])
        spread_bf = sb("spread_bf", [P, TILES * P], BF16)
        we_in = sb("we_in", [P, 2, 3, WSLICE])
        we_hi = sb("we_hi", [P, 3, TILES * P], F32R)
        we_lo = sb("we_lo", [P, 3, TILES * P], F32R)
        ecols_sb = sb("ecols_sb", [P, 3, TILES])
        tanh_g = sb("tanh_g", [P, 2])
        bq_scaled = sb("bq_scaled", [P, 1])
        bo_gated = sb("bo_gated", [P, D])
        half = sb("half", [P, 1])
        xin = sb("xin", [P, RING, 2 * D])
        mask_in = sb("mask_in", [P, RING, 2 * P], I32)
        mask_add = sb("mask_add", [P, RING, 2 * P], BF16)
        stack = sb("stack", [P, RING, 2, H, P], BF16)
        v_one = sb("v_one", [P, RING, H, 32])
        x_bias = sb("x_bias", [P, RING, D])
        bn1 = sb("bn1", [P, 6])
        mv1 = sb("mv1", [P, 2, 2])
        var1 = sb("var1", [P, 1])
        rstd1 = sb("rstd1", [P, 2])
        shift1 = sb("shift1", [P, 2])
        xn = sb("xn", [P, 2, D])
        xn_t = sb("xn_t", [P, P])
        qk = sb("qk", [P, 2 * P])
        qk_rest = sb("qk_rest", [P, 2 * P])
        qk_parts = sb("qk_parts", [P, 2, 2 * PARTS, P], BF16)
        neg_max = sb("neg_max", [P, 2, H])
        max_rest = sb("max_rest", [P, H])
        max_parts = sb("max_parts", [P, PARTS * H], BF16)
        max_t = sb("max_t", [PARTS * H, 2, P], BF16)
        probs = sb("probs", [P, 4, G * P])
        values = sb("values", [P, G * P])
        recip = sb("recip", [P, H])
        attn = sb("attn", [P, D])
        attn_t = sb("attn_t", [P, P])
        x1 = sb("x1", [P, B, D])
        bn2 = sb("bn2", [P, 6])
        mv2 = sb("mv2", [P, 2])
        var2 = sb("var2", [P, 1])
        rstd2 = sb("rstd2", [P, 1])
        xn2 = sb("xn2", [P, D])
        xn2_t = sb("xn2_t", [P, P])
        x_hi = sb("x_hi", [P, B * P], F32R)
        x_lo = sb("x_lo", [P, B * P], F32R)
        logits = sb("logits", [P, B, E])
        r_max = sb("r_max", [P, B])
        r_sum = sb("r_sum", [P, B])
        r_a = sb("r_a", [P, B, E])
        r_score = sb("r_score", [P, B, E])
        r_bias = sb("r_bias", [P, B, E])
        r_pick = sb("r_pick", [P, B, E])
        r_sel = sb("r_sel", [P, 2, B, E])
        weight = sb("weight", [P, B, E + 1])
        weight_rest = sb("weight_rest", [P, B, E + 1])
        weight_parts = sb("weight_parts", [P, B, PARTS, E + 1], BF16)
        weight_t = sb("weight_t", [P, B * P], BF16)
        z3 = sb("z3", [P, 3, CHUNK])
        z = sb("z", [P, 3, CHUNK])
        act = sb("act", [P, 3, CHUNK])
        hid = sb("hid", [P, 3, CHUNK])
        hid_hi = sb("hid_hi", [P, 5, CHUNK], F32R)
        hid_lo = sb("hid_lo", [P, 5, CHUNK], F32R)
        y_t = sb("y_t", [P, CHUNK])

        s_first = sem("s_first")
        s_const = sem("s_const")
        s_experts = sems("s_experts", 2)
        s_pad_q = sem("s_pad_q")
        s_pad_k = sem("s_pad_k")
        s_pad_v = sem("s_pad_v")
        s_half = sem("s_half")
        s_ident = sem("s_ident")
        s_tanh = sem("s_tanh")
        s_bq = sem("s_bq")
        s_bo = sem("s_bo")
        s_spread_in = sem("s_spread_in")
        s_weight_zero = sem("s_weight_zero")
        s_spread_bf = sem("s_spread_bf")
        s_loaded = sems("s_loaded", RING)
        s_bn1 = sem("s_bn1")
        s_stat1 = sem("s_stat1")
        s_var1 = sem("s_var1")
        s_rstd1 = sem("s_rstd1")
        s_shift1 = sem("s_shift1")
        s_xn = sem("s_xn")
        s_mask = sem("s_mask")
        s_xbias = sem("s_xbias")
        s_xn_t = sem("s_xn_t")
        s_xn_t_sb = sem("s_xn_t_sb")
        s_qkv = sem("s_qkv")
        s_qk_sb = sem("s_qk_sb")
        s_v_sb = sem("s_v_sb")
        s_part1 = sem("s_part1")
        s_rest1 = sem("s_rest1")
        s_part2 = sem("s_part2")
        s_parts = sem("s_parts")
        s_scratch = sems("s_scratch", 2)
        s_stack = sems("s_stack", RING)
        s_score = sem("s_score")
        s_max = sem("s_max")
        s_c1 = sem("s_c1")
        s_crest = sem("s_crest")
        s_c2 = sem("s_c2")
        s_c = sem("s_c")
        s_c_t = sem("s_c_t")
        s_c_t_sb = sem("s_c_t_sb")
        s_c_row = sems("s_c_row", RING)
        s_shifted = sem("s_shifted")
        s_exp = sem("s_exp")
        s_value = sem("s_value")
        s_value_sb = sem("s_value_sb")
        s_value_t = sem("s_value_t")
        s_recip = sem("s_recip")
        s_attn = sem("s_attn")
        s_attn_t = sem("s_attn_t")
        s_attn_t_sb = sem("s_attn_t_sb")
        s_proj = sem("s_proj")
        s_x1 = sem("s_x1")
        s_bn2 = sem("s_bn2")
        s_stat2 = sem("s_stat2")
        s_var2 = sem("s_var2")
        s_rstd2 = sem("s_rstd2")
        s_xn2 = sem("s_xn2")
        s_xn2_t = sem("s_xn2_t")
        s_xn2_t_sb = sem("s_xn2_t_sb")
        s_xhi = sem("s_xhi")
        s_xlo = sem("s_xlo")
        s_logit = sem("s_logit")
        s_logit_sb = sem("s_logit_sb")
        s_whi = sem("s_whi")
        s_wlo = sem("s_wlo")
        s_route = sem("s_route")
        s_route_exp = sem("s_route_exp")
        s_weight_t = sem("s_weight_t")
        s_weight_sb = sem("s_weight_sb")
        s_z1 = sem("s_z1")
        s_z3 = sem("s_z3")
        s_spread = sem("s_spread")
        s_z3_sb = sem("s_z3_sb")
        s_z = sem("s_z")
        s_act = sem("s_act")
        s_hid = sem("s_hid")
        s_hid_hi = sem("s_hid_hi")
        s_hid_lo = sem("s_hid_lo")
        s_layer2 = sem("s_layer2")
        s_apart = sem("s_apart")
        s_y_sb = sem("s_y_sb")
        s_y_t = sem("s_y_t")
        s_result = sem("s_result")
        s_out = sem("s_out")

        N_FIRST, N_CONST = 16 * 3, 16 * 3

        ROUTE_STEPS = 24

        def number(b):
            return 4 * b[0] + b[1]

        def place(b, n=RING):
            return b[1] % n

        def used(b, n=RING):
            return b[0] * (4 // n) + b[1] // n

        def after(b, n):
            return (b[0], b[1] + n)

        def exists(b):
            return not isinstance(b[0], int) or number(b) >= 0

        def need(eng, s, value):
            if not isinstance(value, int) or value > 0:
                eng.wait_ge(s, value)

        def apart(eng):
            eng.sem_inc(s_apart, 1)

        def in_bank_pair(m):
            return m % 2

        def twin(m):
            return m % 2 if m < TILES - 1 else 2

        def deep(m):
            return m % 4 if m < TILES - 1 else 4

        def before(c, m, where):
            back = next(d for d in range(1, 2 * TILES) if d == 5 or where((m - d) % TILES) == where(m))
            return TILES * c + m - back + 1

        def walk_tiles(eng, stage, next_stage=None, late=None, finish=None, finish_at=0, beside=None):
            def step(c, m, c_before):
                if m < TILES:
                    stage(c, m)
                if c_before is None:
                    beside(m)
                for part, lag in (next_stage, 1), (late, LAG):
                    if part is not None and m - lag < TILES:
                        if m >= lag:
                            part(c, m - lag)
                        elif c_before is not None:
                            part(c_before, m - lag + TILES)
                if finish is not None:
                    if m == TILES + finish_at:
                        finish(c)
                    elif m == finish_at and c_before is not None:
                        finish(c_before)

            for m in range(TILES):
                step(0, m, None)
            with eng.Fori(0, CHUNKS - 1) as c:
                for m in range(TILES):
                    step(c + 1, m, c)
            for m in range(TILES, TILES + LAG + 3):
                step(CHUNKS - 1, m, CHUNKS - 2)

        block = ctx.enter_context(nc.Block())

        @block.sync
        def _(sp):
            def load(b):
                need(sp, s_xbias, number(b) - RING + 1)
                need(sp, s_mask, number(b) - RING + 1)
                need(sp, s_qkv, number(b) - RING + 1)
                sp.dma_start(xin[:, place(b), :], xc[number(b)]).then_inc(s_loaded[place(b)], 16)
                sp.dma_start(mask_in[:, place(b), :], mk[number(b)]).then_inc(s_loaded[place(b)], 16)

            def store_parts(b):
                sp.wait_ge(s_parts, number(b) + 1)
                apart(sp)
                need(sp, s_stack[place(b)], 48 * used(b))
                sp.dma_start(scratch[place(b), 0:2 * PARTS * DK].rearrange("(n d) (h t) -> (d h) n t", d=DK, h=H),
                             qk_parts[:, place(b, 2)]).then_inc(s_scratch[place(b, 2)], 16)

            def fill_stacks(b):
                sp.wait_ge(s_scratch[place(b, 2)], 16 * used(b, 2) + 16)
                row = 0
                for n in (3, 2, 1):
                    apart_qk = (2 * PARTS - n) * DK
                    src = scratch[place(b), 0:2 * apart_qk].rearrange("(w r) x -> r w x", w=2)[0:n * DK]
                    sp.dma_start(stack[row:row + n * DK, place(b)].rearrange("r w h t -> r w (h t)"), src)\
                        .then_inc(s_stack[place(b)], 16)
                    row += n * DK

            def fill_max_rows(b):
                sp.wait_ge(s_c_t_sb, number(b) + 1)
                sp.dma_start(stack[C_ROW:C_ROW + PARTS, place(b), 0], max_t[:, place(b, 2), :])\
                    .then_inc(s_c_row[place(b)], 16)

            def load_weights(b):
                need(sp, s_wlo, number(b) - 1)
                apart(sp)
                c = bass.ds(number(b) * WSLICE, WSLICE)
                sp.dma_start(we_in[:, place(b, 2)], experts[:, :, c]).then_inc(s_experts[place(b, 2)], 16)

            load((0, 0))
            for dst, src in (ident_sb, ident), (cols_sb, cols), (w_sb, wqkvo):
                sp.dma_start(dst[:], src).then_inc(s_first, 16)
            load((0, 1))
            for dst, src in (rows_sb, rows), (gate_sb, gate_w), (ecols_sb, expert_cols):
                sp.dma_start(dst[:], src).then_inc(s_const, 16)
            load((0, 2))
            load((0, 3))
            sp.dma_start(spread_sb[:], spread).then_inc(s_spread_in, 16)

            def padded(n):
                sp.wait_ge(s_pad_q, 2 * n)
                sp.wait_ge(s_pad_k, 3 * n)

            store_parts((0, 0))
            padded(1)
            fill_stacks((0, 0))
            store_parts((0, 1))
            padded(2)
            store_parts((0, 2))
            fill_stacks((0, 1))
            fill_max_rows((0, 0))
            load_weights((0, 0))
            padded(RING)

            def step(s, nxt=True, new=True, stack2=True, more=True):
                if more:
                    load(after(s, 4))
                if stack2:
                    fill_stacks(after(s, 2))
                if nxt:
                    fill_max_rows(after(s, 1))
                    load_weights(after(s, 1))
                if new:
                    store_parts(after(s, 3))

            with sp.Fori(0, 3) as i:
                for j in range(4):
                    step((i, j))
            step((3, 0), more=False)
            step((3, 1), more=False, new=False)
            step((3, 2), more=False, new=False, stack2=False)

            with sp.Fori(0, CHUNKS) as c:
                sp.wait_ge(s_result, c + 1)
                apart(sp)
                sp.dma_start(out.rearrange("(n p) d -> p n d", p=P)[:, bass.ds(4 * c, 4), :],
                             x1[:, bass.ds(4 * c, 4), :]).then_inc(s_out, 16)
            sp.wait_ge(s_out, 16 * CHUNKS)

        @block.gpsimd
        def _(pool):
            def pad_k(n):
                for m, (a, b, value) in enumerate(((32, 64, 0.0), (64, 96, 0.0), (96, 128, BF16_ONES))):
                    pool.memset(stack[a:b, n, 1].rearrange("p h t -> p (h t)").bitcast(F32), value).then_inc(s_pad_k, 1)
                    pool.wait_ge(s_pad_k, 3 * n + m + 1)

            pool.memset(half[:], -0.5).then_inc(s_half, 1)
            pool.memset(v_one[:], 0.0).then_inc(s_pad_v, 1)
            pool.wait_ge(s_pad_v, 1)
            pool.memset(v_one[:, :, :, DK:DK + 1], 1.0).then_inc(s_pad_v, 1)
            pool.wait_ge(s_half, 1)

            def scale1(b):
                pool.wait_ge(s_stat1, number(b) + 1)
                apart(pool)
                pool.tensor_scalar(var1[:], mv1[:, place(b, 2), 1:2], EPS, None, ALU.add).then_inc(s_var1, 1)
                pool.wait_ge(s_var1, number(b) + 1)
                need(pool, s_xn, number(b) - 1)
                k = slice(place(b, 2), place(b, 2) + 1)
                apart(pool)
                pool.tensor_tensor(rstd1[:, k], var1[:], half[:], ALU.pow).then_inc(s_rstd1, 1)
                pool.wait_ge(s_rstd1, number(b) + 1)
                apart(pool)
                pool.tensor_scalar(shift1[:, k], mv1[:, place(b, 2), 0:1], rstd1[:, k], -1.0,
                                   ALU.mult, ALU.mult).then_inc(s_shift1, 1)

            def bias_x(b):
                need(pool, s_x1, number(b) - RING + 1)
                pool.tensor_tensor(x_bias[:, place(b), :], xin[:, place(b), 0:D], bo_gated[:], ALU.add)\
                    .then_inc(s_xbias, 1)

            def cut_max(b):
                pool.wait_ge(s_max, 4 * number(b) + 4)
                need(pool, s_c_t, number(b))
                m = neg_max[:, place(b, 2), :]
                apart(pool)
                pool.tensor_copy(max_parts[:, 0:H], m).then_inc(s_c1, 1)
                pool.wait_ge(s_c1, number(b) + 1)
                pool.tensor_tensor(max_rest[:], m, max_parts[:, 0:H], ALU.subtract).then_inc(s_crest, 1)
                pool.wait_ge(s_crest, number(b) + 1)
                apart(pool)
                pool.tensor_copy(max_parts[:, H:2 * H], max_rest[:]).then_inc(s_c2, 1)
                pool.wait_ge(s_c2, number(b) + 1)
                pool.tensor_tensor(max_parts[:, 2 * H:3 * H], max_rest[:], max_parts[:, H:2 * H], ALU.subtract)\
                    .then_inc(s_c, 1)

            def scale2(b):
                pool.wait_ge(s_stat2, number(b) + 1)
                need(pool, s_xn2, number(b))
                apart(pool)
                pool.tensor_scalar(var2[:], mv2[:, 1:2], EPS, None, ALU.add).then_inc(s_var2, 1)
                pool.wait_ge(s_var2, number(b) + 1)
                pool.tensor_tensor(rstd2[:], var2[:], half[:], ALU.pow).then_inc(s_rstd2, 1)

            def slice_of(b):
                return bass.ds(number(b) * WSLICE, WSLICE)

            def weights_hi(b):
                pool.wait_ge(s_experts[place(b, 2)], 16 * used(b, 2) + 16)
                apart(pool)
                pool.tensor_copy(we_hi[:, :, slice_of(b)], we_in[:, place(b, 2)]).then_inc(s_whi, 1)

            def weights_lo(b):
                pool.wait_ge(s_whi, number(b) + 1)
                pool.tensor_tensor(we_lo[:, :, slice_of(b)], we_in[:, place(b, 2)], we_hi[:, :, slice_of(b)],
                                   ALU.subtract).then_inc(s_wlo, 1)

            def x_lo_part(b):
                pool.wait_ge(s_xhi, number(b) + 1)
                c = bass.ds(number(b) * P, P)
                pool.tensor_tensor(x_lo[:, c], xn2_t[:], x_hi[:, c], ALU.subtract).then_inc(s_xlo, 1)

            scale1((0, 0))
            pool.wait_ge(s_first, N_FIRST)
            pool.tensor_scalar(bq_scaled[:], cols_sb[:, 0:1], QSCALE, None, ALU.mult).then_inc(s_bq, 1)
            pool.wait_ge(s_bq, 1)
            pad_k(0)
            scale1((0, 1))
            pool.tensor_copy(ident_bf[:], ident_sb[:]).then_inc(s_ident, 1)
            scale1((0, 2))
            pool.wait_ge(s_shift1, 3)
            pad_k(1)
            pad_k(2)
            pad_k(3)
            cut_max((0, 0))
            pool.wait_ge(s_tanh, 1)
            pool.wait_ge(s_const, N_CONST)
            pool.tensor_scalar(bo_gated[:], rows_sb[:, 0:D], tanh_g[:, 0:1], None, ALU.mult).then_inc(s_bo, 1)
            pool.wait_ge(s_bo, 1)
            for j in range(3):
                bias_x((0, j))

            def step(s, prev=True, nxt=True, new=True):
                if new:
                    scale1(after(s, 3))
                weights_hi(s)
                if nxt:
                    cut_max(after(s, 1))
                if prev:
                    scale2(after(s, -1))
                if new:
                    bias_x(after(s, 3))
                weights_lo(s)
                if prev:
                    x_lo_part(after(s, -1))

            step((0, 0), prev=False)
            with pool.Fori(0, 3) as i:
                for j in range(1, 5):
                    step((i, j))
            step((3, 1), new=False)
            step((3, 2), new=False)
            step((3, 3), new=False, nxt=False)

            def cut_hidden(c, m):
                n = TILES * c + m
                pool.wait_ge(s_hid_hi, n + 1)
                need(pool, s_layer2, before(c, m, deep))
                pool.tensor_tensor(hid_lo[:, deep(m)], hid[:, twin(m)], hid_hi[:, deep(m)], ALU.subtract)\
                    .then_inc(s_hid_lo, 1)

            def beside(m):
                if m == 0:
                    scale2((3, 3))
                if m == 4:
                    x_lo_part((3, 3))

            walk_tiles(pool, cut_hidden, beside=beside)

        @block.scalar
        def _(act_e):
            def normalise(b):
                act_e.wait_ge(s_shift1, number(b) + 1)
                need(act_e, s_xn_t, number(b) - 1)
                k = slice(place(b, 2), place(b, 2) + 1)
                act_e.activation(xn[:, place(b, 2), :], xin[:, place(b), 0:D], ACT.Identity, bias=shift1[:, k],
                                 scale=rstd1[:, k]).then_inc(s_xn, 1)

            def copy_xn_t(b):
                act_e.wait_ge(s_xn_t, number(b) + 1)
                need(act_e, s_qkv, number(b))
                act_e.activation(xn_t[:], in_bank[:, 384:512], ACT.Copy).then_inc(s_xn_t_sb, 1)

            def copy_qk(b):
                act_e.wait_ge(s_qkv, number(b) + 1)
                need(act_e, s_rest1, number(b))
                act_e.activation(qk[:, 0:P], in_bank[:, 0:P], ACT.Identity, bias=bq_scaled[:, 0:1],
                                 scale=QSCALE).then_inc(s_qk_sb, 1)
                act_e.activation(qk[:, P:2 * P], in_bank[:, P:2 * P], ACT.Identity, bias=cols_sb[:, 1:2])\
                    .then_inc(s_qk_sb, 1)

            def copy_v(b):
                need(act_e, s_value, 4 * number(b) - 4 * (RING - 1))
                act_e.activation(v_one[:, place(b), :, 0:DK],
                                 in_bank[:, 256:384].rearrange("p (h d) -> p h d", d=DK), ACT.Copy)\
                    .then_inc(s_v_sb, 1)

            def copy_max_t(b):
                act_e.wait_ge(s_c_t, number(b) + 1)
                o = after(b, -2)
                if exists(o):
                    act_e.wait_ge(s_c_row[place(o)], 16 * used(o) + 16)
                act_e.activation(max_t[:, place(b, 2), :], turn_bank[0:PARTS * H, 0:P // 2].bitcast(BF16), ACT.Copy)\
                    .then_inc(s_c_t_sb, 1)

            def exp(b, g):
                act_e.wait_ge(s_shifted, 4 * number(b) + g + 1)
                need(act_e, s_value, 4 * number(b) + g - 3)
                act_e.activation(probs[:, g, :], prob_bank[g % 2][:, :], ACT.Exp).then_inc(s_exp, 1)

            def copy_values(b):
                act_e.wait_ge(s_value, 4 * number(b) + 4)
                need(act_e, s_value_t, number(b))
                act_e.activation(values[:], value_bank[:, :], ACT.Copy).then_inc(s_value_sb, 1)

            def copy_attn_t(b):
                act_e.wait_ge(s_attn_t, number(b) + 1)
                need(act_e, s_proj, number(b))
                act_e.activation(attn_t[:], out_bank[:, 0:P], ACT.Identity, bias=cols_sb[:, 2:3])\
                    .then_inc(s_attn_t_sb, 1)

            def copy_xn2_t(b):
                act_e.wait_ge(s_xn2_t, number(b) + 1)
                need(act_e, s_logit, number(b))
                need(act_e, s_xlo, number(b))
                act_e.activation(xn2_t[:], out_bank[:, 0:P], ACT.Copy).then_inc(s_xn2_t_sb, 1)
                act_e.activation(x_hi[:, bass.ds(number(b) * P, P)], out_bank[:, 0:P], ACT.Copy).then_inc(s_xhi, 1)

            def copy_logits(b):
                act_e.wait_ge(s_logit, number(b) + 1)
                act_e.activation(logits[:, bass.ds(number(b), 1), :].rearrange("p n e -> p (n e)"),
                                 out_bank[:, 0:E], ACT.Copy).then_inc(s_logit_sb, 1)

            normalise((0, 0))
            copy_xn_t((0, 0))
            act_e.wait_ge(s_bq, 1)
            copy_qk((0, 0))
            act_e.wait_ge(s_pad_v, 2)
            copy_v((0, 0))
            act_e.activation(tanh_g[:], cols_sb[:, 3:5], ACT.Tanh).then_inc(s_tanh, 1)
            normalise((0, 1))
            copy_xn_t((0, 1))
            copy_qk((0, 1))
            copy_v((0, 1))
            normalise((0, 2))
            copy_xn_t((0, 2))
            copy_qk((0, 2))
            copy_v((0, 2))
            act_e.wait_ge(s_spread_in, 16)
            act_e.activation(spread_bf[:], spread_sb[:], ACT.Copy).then_inc(s_spread_bf, 1)
            copy_max_t((0, 0))

            def route_exp(group):
                n = slice(0, EARLY) if group == 0 else slice(EARLY, B)
                act_e.wait_ge(s_route, ROUTE_STEPS * group + 2)
                act_e.activation(r_a[:, n], r_a[:, n], ACT.Exp).then_inc(s_route_exp, 1)

            def copy_weights(count, first, entries, turned):
                act_e.wait_ge(s_weight_t, count)
                act_e.wait_ge(s_weight_zero, 1)
                act_e.activation(weight_t[0:PARTS * (E + 1), first * P:(first + entries) * P],
                                 turned[0:PARTS * (E + 1), 0:entries * P // 2].bitcast(BF16), ACT.Copy)\
                    .then_inc(s_weight_sb, 1)

            def step(s, prev=True, nxt=True, new=True, route=False):
                if new:
                    normalise(after(s, 3))
                    copy_xn_t(after(s, 3))
                if prev:
                    copy_attn_t(after(s, -1))
                exp(s, 0)
                exp(s, 1)
                if route:
                    route_exp(0)
                if new:
                    copy_qk(after(s, 3))
                    copy_v(after(s, 3))
                exp(s, 2)
                if nxt:
                    copy_max_t(after(s, 1))
                exp(s, 3)
                if prev:
                    copy_xn2_t(after(s, -1))
                copy_values(s)
                if prev:
                    copy_logits(after(s, -1))

            step((0, 0), prev=False)
            with act_e.Fori(0, 3) as i:
                for j in range(1, 5):
                    step((i, j))
            step((3, 1), new=False, route=True)
            step((3, 2), new=False)
            exp((3, 3), 0)
            exp((3, 3), 1)
            copy_attn_t((3, 2))
            exp((3, 3), 2)
            exp((3, 3), 3)
            copy_values((3, 3))
            copy_weights(2, 8, 4, turn_bank)
            act_e.wait_ge(s_const, N_CONST)

            def copy_z3(c, m):
                act_e.wait_ge(s_z3, TILES * c + m + 1)
                need(act_e, s_z, before(c, m, twin))
                act_e.activation(z3[:, twin(m)], z3_bank[in_bank_pair(m)][:, :], ACT.Identity,
                                 bias=ecols_sb[:, 1, m:m + 1]).then_inc(s_z3_sb, 1)

            def silu(c, m):
                act_e.wait_ge(s_z, TILES * c + m + 1)
                need(act_e, s_hid, before(c, m, twin))
                act_e.activation(act[:, twin(m)], z[:, twin(m)], ACT.Silu).then_inc(s_act, 1)

            def copy_y(c):
                act_e.wait_ge(s_layer2, TILES * c + TILES)
                act_e.activation(y_t[:], y_bank[:, :], ACT.Copy, scale=tanh_g[:, 1:2]).then_inc(s_y_sb, 1)

            def beside(m):
                if m == 0:
                    copy_xn2_t((3, 2))
                if m == 1:
                    copy_logits((3, 2))
                    copy_attn_t((3, 3))
                if m == 4:
                    copy_xn2_t((3, 3))
                if m == 5:
                    copy_logits((3, 3))
                if m == 6:
                    route_exp(1)
                if m == TILES - 1:
                    copy_weights(3, EARLY, 4, yt_bank)

            walk_tiles(act_e, copy_z3, silu, None, copy_y, LAG - 1, beside)

        @block.vector
        def _(dve):
            def stats1(b):
                dve.wait_ge(s_loaded[place(b)], 32 * used(b) + 32)
                need(dve, s_stat1, number(b))
                dve.bn_stats(bn1[:], xin[:, place(b), 0:D]).then_inc(s_bn1, 1)
                dve.wait_ge(s_bn1, number(b) + 1)
                need(dve, s_shift1, number(b) - 1)
                apart(dve)
                dve.bn_aggr(mv1[:, place(b, 2), :], bn1[:]).then_inc(s_stat1, 1)

            def add_of_mask(b):
                dve.wait_ge(s_loaded[place(b)], 32 * used(b) + 32)
                need(dve, s_shifted, 4 * number(b) - 4 * (RING - 1))
                apart(dve)
                dve.tensor_scalar(mask_add[:, place(b), :], mask_in[:, place(b), :], 0.0, MASKED,
                                  ALU.is_equal, ALU.mult).then_inc(s_mask, 1)

            def part(b, i):
                return qk_parts[:, place(b, 2), i:2 * PARTS - i:2 * PARTS - 1 - 2 * i]

            qk_pair = qk[:].rearrange("p (w t) -> p w t", w=2)
            rest_pair = qk_rest[:].rearrange("p (w t) -> p w t", w=2)

            def cut1(b):
                dve.wait_ge(s_qk_sb, 2 * number(b) + 2)
                need(dve, s_scratch[place(b, 2)], 16 * used(b, 2))
                dve.tensor_copy(part(b, 0), qk_pair).then_inc(s_part1, 1)

            def cut2(b):
                dve.wait_ge(s_part1, number(b) + 1)
                dve.tensor_tensor(rest_pair, qk_pair, part(b, 0), ALU.subtract).then_inc(s_rest1, 1)

            def cut3(b):
                dve.wait_ge(s_rest1, number(b) + 1)
                dve.tensor_copy(part(b, 1), rest_pair).then_inc(s_part2, 1)

            def cut4(b):
                dve.wait_ge(s_part2, number(b) + 1)
                dve.tensor_tensor(part(b, 2), rest_pair, part(b, 1), ALU.subtract).then_inc(s_parts, 1)

            def cut_qk(b):
                for cut in (cut1, cut2, cut3, cut4):
                    cut(b)

            def row_max(b, g):
                dve.wait_ge(s_score, 4 * number(b) + g + 1)
                if g == 0:
                    need(dve, s_c, number(b) - 1)
                dve.tensor_reduce(neg_max[:, place(b, 2), G * g:G * g + G],
                                  score_bank[g % 2][:, :].rearrange("p (h k) -> p h k", h=G), AX.X, ALU.max,
                                  negate=True).then_inc(s_max, 1)

            def divide(b):
                dve.wait_ge(s_value_t, number(b) + 1)
                t = turn_bank[:, :].rearrange("p (h c) -> p h c", c=32)
                dve.reciprocal(recip[:].rearrange("p (h c) -> p h c", c=1), t[:, :, DK:DK + 1]).then_inc(s_recip, 1)
                dve.wait_ge(s_recip, number(b) + 1)
                need(dve, s_attn_t, number(b))
                dve.tensor_tensor(attn[:].rearrange("p (h d) -> p h d", d=DK), t[:, :, 0:DK],
                                  recip[:].rearrange("p (h c) -> p h c", c=1).broadcast_to([P, H, DK]),
                                  ALU.mult).then_inc(s_attn, 1)

            def residual(b):
                dve.wait_ge(s_proj, number(b) + 1)
                dve.wait_ge(s_xbias, number(b) + 1)
                x1_b = x1[:, bass.ds(number(b), 1), :].rearrange("p n d -> p (n d)")
                dve.scalar_tensor_tensor(x1_b, out_bank[:, 0:D], tanh_g[:, 0:1], x_bias[:, place(b), :],
                                         ALU.mult, ALU.add).then_inc(s_x1, 1)
                dve.wait_ge(s_x1, number(b) + 1)
                apart(dve)
                dve.bn_stats(bn2[:], x1_b).then_inc(s_bn2, 1)

            def stats2(b):
                dve.wait_ge(s_bn2, number(b) + 1)
                need(dve, s_xn2, number(b))
                apart(dve)
                dve.bn_aggr(mv2[:], bn2[:]).then_inc(s_stat2, 1)

            def normalise2(b):
                dve.wait_ge(s_rstd2, number(b) + 1)
                need(dve, s_xn2_t, number(b))
                dve.tensor_scalar(xn2[:], x1[:, bass.ds(number(b), 1), :].rearrange("p n d -> p (n d)"),
                                  mv2[:, 0:1], rstd2[:], ALU.subtract, ALU.mult).then_inc(s_xn2, 1)

            def pad_q(n):
                for a, b in ((32, 64), (64, 128)):
                    dve.memset(stack[a:b, n, 0].rearrange("p h t -> p (h t)").bitcast(F32), 0.0).then_inc(s_pad_q, 1)

            pad_q(0)
            stats1((0, 0))
            add_of_mask((0, 0))
            pad_q(1)
            stats1((0, 1))
            pad_q(2)
            cut_qk((0, 0))
            add_of_mask((0, 1))
            stats1((0, 2))
            pad_q(3)
            cut_qk((0, 1))
            add_of_mask((0, 2))
            cut_qk((0, 2))
            for g in range(4):
                row_max((0, 0), g)
            dve.memset(weight_t[:], 0.0).then_inc(s_weight_zero, 1)

            def route(group, first, last):
                n = slice(0, EARLY) if group == 0 else slice(EARLY, B)

                def col(t):
                    return t[:, n].rearrange("p (n c) -> p n c", c=1).broadcast_to([P, n.stop - n.start, E])

                def row(t):
                    return t.rearrange("p (n e) -> p n e", n=1).broadcast_to([P, n.stop - n.start, E])

                for k in range(first, last + 1):
                    if k == 0:
                        dve.wait_ge(s_const, N_CONST)
                        dve.wait_ge(s_logit_sb, n.stop)
                    if group or k:
                        dve.wait_ge(s_route, ROUTE_STEPS * group + k)
                    if k == 0:
                        op = dve.tensor_reduce(r_max[:, n], logits[:, n], AX.X, ALU.max)
                    elif k == 1:
                        op = dve.tensor_tensor(r_a[:, n], logits[:, n], col(r_max), ALU.subtract)
                    elif k == 2:
                        dve.wait_ge(s_route_exp, group + 1)
                        op = dve.tensor_reduce(r_sum[:, n], r_a[:, n], AX.X, ALU.add)
                    elif k == 3:
                        op = dve.reciprocal(r_sum[:, n], r_sum[:, n])
                    elif k == 4:
                        op = dve.tensor_tensor(r_score[:, n], r_a[:, n], col(r_sum), ALU.mult)
                    elif k == 5:
                        op = dve.tensor_tensor(r_bias[:, n], r_score[:, n], row(rows_sb[:, D:D + E]), ALU.add)
                    elif k in (6, 12):
                        op = dve.tensor_reduce(r_max[:, n], r_bias[:, n], AX.X, ALU.max)
                    elif k in (7, 13):
                        op = dve.tensor_tensor(r_pick[:, n], r_bias[:, n], col(r_max), ALU.is_equal)
                    elif k in (8, 14):
                        op = dve.tensor_tensor(r_pick[:, n], r_pick[:, n], row(rows_sb[:, D + E:D + 2 * E]), ALU.mult)
                    elif k in (9, 15):
                        op = dve.tensor_reduce(r_max[:, n], r_pick[:, n], AX.X, ALU.max)
                    elif k in (10, 16):
                        op = dve.tensor_tensor(r_sel[:, k // 16, n], r_pick[:, n], col(r_max), ALU.is_equal)
                    elif k == 11:
                        op = dve.scalar_tensor_tensor(r_bias[:, n], r_sel[:, 0, n], -3e38, r_bias[:, n],
                                                      ALU.mult, ALU.add)
                    elif k == 17:
                        op = dve.tensor_tensor(r_pick[:, n], r_sel[:, 0, n], r_sel[:, 1, n], ALU.add)
                    elif k == 18:
                        op = dve.memset(weight[:, n, E:E + 1], 1.0)
                    elif k == 19:
                        op = dve.tensor_tensor(weight[:, n, 0:E], r_score[:, n], r_pick[:, n], ALU.mult)
                    elif k == 20:
                        op = dve.tensor_copy(weight_parts[:, n, 0], weight[:, n])
                    elif k == 21:
                        op = dve.tensor_tensor(weight_rest[:, n], weight[:, n], weight_parts[:, n, 0], ALU.subtract)
                    elif k == 22:
                        op = dve.tensor_copy(weight_parts[:, n, 1], weight_rest[:, n])
                    elif k == 23:
                        op = dve.tensor_tensor(weight_parts[:, n, 2], weight_rest[:, n], weight_parts[:, n, 1],
                                               ALU.subtract)
                    op.then_inc(s_route, 1)

            def step(s, prev=True, nxt=True, new=True, routing=False):
                p, n, w = after(s, -1), after(s, 1), after(s, 3)
                if new:
                    stats1(w)
                if nxt:
                    row_max(n, 0)
                    row_max(n, 1)
                if prev:
                    divide(p)
                if nxt:
                    row_max(n, 2)
                    row_max(n, 3)
                if new:
                    add_of_mask(w)
                if routing:
                    route(0, 0, 1)
                if prev:
                    residual(p)
                    stats2(p)
                if routing:
                    route(0, 2, 5)
                if new:
                    cut1(w)
                    cut2(w)
                if prev:
                    normalise2(p)
                if new:
                    cut3(w)
                    cut4(w)

            dve.wait_ge(s_tanh, 1)
            step((0, 0), prev=False)
            with dve.Fori(0, 3) as i:
                for j in range(1, 5):
                    step((i, j))
            step((3, 1), new=False, routing=True)
            route(0, 6, 11)
            step((3, 2), new=False)
            route(0, 12, 16)
            divide((3, 2))
            route(0, 17, 23)
            residual((3, 2))
            stats2((3, 2))
            dve.wait_ge(s_weight_t, 1)
            dve.wait_ge(s_weight_zero, 1)
            dve.tensor_copy(weight_t[0:PARTS * (E + 1), 0:8 * P],
                            in_bank[0:PARTS * (E + 1), :].bitcast(BF16)).then_inc(s_weight_sb, 1)
            normalise2((3, 2))

            def gate(c, m):
                n = TILES * c + m
                dve.wait_ge(s_z1, n + 1)
                dve.wait_ge(s_z3_sb, n + 1)
                need(dve, s_act, before(c, m, twin))
                dve.scalar_tensor_tensor(z[:, twin(m)], z1_bank[in_bank_pair(m)][:, :], ecols_sb[:, 0, m:m + 1],
                                         z3[:, twin(m)], ALU.add, ALU.mult).then_inc(s_z, 1)

            def weigh(c, m):
                n = TILES * c + m
                dve.wait_ge(s_act, n + 1)
                dve.wait_ge(s_spread, n + 1)
                need(dve, s_hid_lo, before(c, m, twin))
                dve.scalar_tensor_tensor(hid[:, twin(m)], act[:, twin(m)], ecols_sb[:, 2, m:m + 1],
                                         spread_bank[in_bank_pair(m)][:, :], ALU.add, ALU.mult).then_inc(s_hid, 1)
                if isinstance(c, int) and c == 0 and 6 <= m < 11:
                    route(1, 4 * m - 20, 4 * m - 19 if m < 10 else ROUTE_STEPS - 1)
                dve.wait_ge(s_hid, n + 1)
                need(dve, s_layer2, before(c, m, deep))
                dve.tensor_copy(hid_hi[:, deep(m)], hid[:, twin(m)]).then_inc(s_hid_hi, 1)

            def finish(c):
                dve.wait_ge(s_y_t, c + 1)
                x1_c = x1[:, bass.ds(4 * c, 4), :].rearrange("p n d -> p (n d)")
                dve.tensor_tensor(x1_c, yt_bank[:, :], x1_c, ALU.add).then_inc(s_result, 1)

            def beside(m):
                if m == 0:
                    divide((3, 3))
                if m == 2:
                    residual((3, 3))
                    stats2((3, 3))
                if m == 3:
                    normalise2((3, 3))
                if m == 6:
                    route(1, 0, 1)
                if 7 <= m < 12:
                    route(1, 4 * m - 26, 4 * m - 25)

            walk_tiles(dve, gate, weigh, None, finish, LAG + 2, beside)

        @block.tensor
        def _(pe):
            def turn_xn(b):
                pe.wait_ge(s_xn, number(b) + 1)
                need(pe, s_v_sb, number(b))
                pe.transpose(in_bank[:, 384:512], xn[:, place(b, 2), :], ident_sb[:]).then_inc(s_xn_t, 1)

            def project_in(b):
                pe.wait_ge(s_xn_t_sb, number(b) + 1)
                ctx_t = xin[:, place(b), D:2 * D]
                pe.matmul(in_bank[:, 0:P], w_sb[:, 0:D], xn_t[:], start=True, stop=True)
                pe.matmul(in_bank[:, P:2 * P], w_sb[:, D:2 * D], ctx_t, start=True, stop=True)
                pe.matmul(in_bank[:, 2 * P:3 * P], ctx_t, w_sb[:, 2 * D:3 * D], start=True, stop=True)\
                    .then_inc(s_qkv, 1)

            def scores(b, g):
                if g == 0:
                    pe.wait_ge(s_stack[place(b)], 48 * used(b) + 48)
                    pe.wait_ge(s_mask, number(b) + 1)
                need(pe, s_max, 4 * number(b) + g - 1)
                o = score_bank[g % 2]
                for n in range(G):
                    pe.matmul(o[:, n * P:(n + 1) * P], stack[0:C_ROW, place(b), 0, G * g + n, :],
                              stack[0:C_ROW, place(b), 1, G * g + n, :], start=n == 0, stop=False,
                              skip_group_check=True)
                pe.matmul(o[:, :].rearrange("p (n k) -> p n k", n=G), ident_bf[:],
                          mask_add[:, place(b), 0:P].rearrange("p (n k) -> p n k", n=1).broadcast_to([P, G, P]),
                          start=False, stop=True, skip_group_check=True).then_inc(s_score, 1)

            def shifted(b, g):
                if g == 0:
                    pe.wait_ge(s_c_row[place(b)], 16 * used(b) + 16)
                need(pe, s_exp, 4 * number(b) + g - 1)
                o = prob_bank[g % 2]
                for n in range(G):
                    pe.matmul(o[:, n * P:(n + 1) * P], stack[:, place(b), 1, G * g + n, :],
                              stack[:, place(b), 0, G * g + n, :], start=n == 0, stop=False,
                              skip_group_check=True)
                pe.matmul(o[:, :].rearrange("p (n k) -> p n k", n=G), ident_bf[:],
                          mask_add[:, place(b), P:2 * P].rearrange("p (n k) -> p n k", n=1).broadcast_to([P, G, P]),
                          start=False, stop=True, skip_group_check=True).then_inc(s_shifted, 1)

            def weigh_values(b, g):
                pe.wait_ge(s_exp, 4 * number(b) + g + 1)
                if g == 0:
                    pe.wait_ge(s_v_sb, number(b) + 1)
                    need(pe, s_value_sb, number(b))
                for n in range(G):
                    mm = pe.matmul(value_bank[32 * n:32 * n + 32, g * P:(g + 1) * P], v_one[:, place(b), G * g + n, :],
                                   probs[:, g, n * P:(n + 1) * P], start=True, stop=True)
                mm.then_inc(s_value, 1)

            def turn_values(b):
                pe.wait_ge(s_value_sb, number(b) + 1)
                pe.wait_ge(s_c_t_sb, number(b) + 2 if not isinstance(b[0], int) else min(number(b) + 2, B))
                for g in range(4):
                    t = pe.transpose(turn_bank[:, g * P:(g + 1) * P], values[:, g * P:(g + 1) * P], ident_sb[:])
                t.then_inc(s_value_t, 1)

            def turn_attn(b):
                pe.wait_ge(s_attn, number(b) + 1)
                need(pe, s_logit_sb, number(b))
                pe.transpose(out_bank[:, 0:P], attn[:], ident_sb[:]).then_inc(s_attn_t, 1)

            def project_out(b):
                pe.wait_ge(s_attn_t_sb, number(b) + 1)
                pe.matmul(out_bank[:, 0:P], attn_t[:], w_sb[:, 3 * D:4 * D], start=True, stop=True)\
                    .then_inc(s_proj, 1)

            def turn_max(b):
                pe.wait_ge(s_c, number(b) + 1)
                need(pe, s_attn, number(b) - 1)
                apart(pe)
                pe.transpose(turn_bank[0:PARTS * H, 0:P // 2].bitcast(BF16), max_parts[:], ident_bf[:]).then_inc(s_c_t, 1)

            def turn_xn2(b):
                pe.wait_ge(s_xn2, number(b) + 1)
                pe.transpose(out_bank[:, 0:P], xn2[:], ident_sb[:]).then_inc(s_xn2_t, 1)

            def route(b):
                pe.wait_ge(s_xhi, number(b) + 1)
                pe.matmul(out_bank[:, 0:E], xn2_t[:], gate_sb[:], start=True, stop=True).then_inc(s_logit, 1)

            pe.wait_ge(s_first, N_FIRST)
            turn_xn((0, 0))
            project_in((0, 0))
            turn_xn((0, 1))
            project_in((0, 1))
            turn_xn((0, 2))
            project_in((0, 2))
            pe.wait_ge(s_ident, 1)
            for g in range(4):
                scores((0, 0), g)
            turn_max((0, 0))
            pe.wait_ge(s_const, N_CONST)

            def step(s, prev=True, nxt=True, new=True, ahead=True):
                p, n, w = after(s, -1), after(s, 1), after(s, 3)
                if nxt:
                    scores(n, 2)
                    scores(n, 3)
                if new:
                    turn_xn(w)
                if prev:
                    turn_attn(p)
                shifted(s, 0)
                shifted(s, 1)
                if prev:
                    project_out(p)
                if new:
                    project_in(w)
                weigh_values(s, 0)
                shifted(s, 2)
                if nxt:
                    turn_max(n)
                weigh_values(s, 1)
                shifted(s, 3)
                weigh_values(s, 2)
                if prev:
                    turn_xn2(p)
                weigh_values(s, 3)
                if ahead:
                    scores(after(s, 2), 0)
                    scores(after(s, 2), 1)
                if prev:
                    route(p)
                turn_values(s)

            scores((0, 1), 0)
            scores((0, 1), 1)
            step((0, 0), prev=False)
            with pe.Fori(0, 3) as i:
                for j in range(1, 5):
                    step((i, j))
            step((3, 1), new=False)
            step((3, 2), new=False, ahead=False)

            def turn_weights(first, entries, into):
                for t in range(entries):
                    tr = pe.transpose(into[0:PARTS * (E + 1), 64 * t:64 * t + 64].bitcast(BF16),
                                      weight_parts[:, first + t].rearrange("p i e -> p (i e)"), ident_bf[:])
                tr.then_inc(s_weight_t, 1)

            shifted((3, 3), 0)
            shifted((3, 3), 1)
            weigh_values((3, 3), 0)
            turn_attn((3, 2))
            shifted((3, 3), 2)
            weigh_values((3, 3), 1)
            shifted((3, 3), 3)
            project_out((3, 2))
            pe.wait_ge(s_route, ROUTE_STEPS)
            turn_weights(0, 8, in_bank)
            weigh_values((3, 3), 2)
            turn_weights(8, 4, turn_bank)
            weigh_values((3, 3), 3)
            pe.wait_ge(s_spread_bf, 1)
            pe.wait_ge(s_wlo, 13)
            pe.wait_ge(s_xlo, EARLY)
            pe.wait_ge(s_exp, 4 * B)
            pe.wait_ge(s_v_sb, B)

            def layer1(c, m):
                cols_m = slice(m * P, (m + 1) * P)
                tok = bass.ds(c * CHUNK, CHUNK)
                k = in_bank_pair(m)
                for w, o, done, read in ((1, z3_bank[k], s_z3, s_z3_sb), (0, z1_bank[k], s_z1, s_z)):
                    need(pe, read, before(c, m, in_bank_pair))
                    pe.matmul(o[:, :], we_hi[:, w, cols_m], x_hi[:, tok], start=True, stop=False)
                    pe.matmul(o[:, :], we_hi[:, w, cols_m], x_lo[:, tok], start=False, stop=False)
                    pe.matmul(o[:, :], we_lo[:, w, cols_m], x_hi[:, tok], start=False, stop=True).then_inc(done, 1)

            def spread_weights(c, m):
                k = in_bank_pair(m)
                need(pe, s_hid, before(c, m, in_bank_pair))
                pe.matmul(spread_bank[k][:, :], spread_bf[:, m * P:(m + 1) * P], weight_t[:, bass.ds(c * CHUNK, CHUNK)],
                          start=True, stop=True).then_inc(s_spread, 1)

            def layer2(c, m):
                n = TILES * c + m
                cols_m = slice(m * P, (m + 1) * P)
                pe.wait_ge(s_hid_lo, n + 1)
                if m == 0:
                    need(pe, s_y_sb, c)
                pe.matmul(y_bank[:, :], we_hi[:, 2, cols_m], hid_hi[:, deep(m)], start=m == 0, stop=False)
                pe.matmul(y_bank[:, :], we_lo[:, 2, cols_m], hid_hi[:, deep(m)], start=False, stop=False)
                pe.matmul(y_bank[:, :], we_hi[:, 2, cols_m], hid_lo[:, deep(m)], start=False, stop=m == TILES - 1)\
                    .then_inc(s_layer2, 1)

            def turn_y(c):
                pe.wait_ge(s_y_sb, c + 1)
                for t in range(CHUNK // P):
                    tr = pe.transpose(yt_bank[:, t * P:(t + 1) * P], y_t[:, t * P:(t + 1) * P], ident_sb[:])
                tr.then_inc(s_y_t, 1)

            def beside(m):
                if m == 0:
                    turn_xn2((3, 2))
                    pe.wait_ge(s_weight_sb, 2)
                    turn_values((3, 3))
                if m == 1:
                    route((3, 2))
                    turn_attn((3, 3))
                if m == 2:
                    project_out((3, 3))
                if m == 4:
                    turn_xn2((3, 3))
                if m == 5:
                    route((3, 3))
                if m == 9:
                    pe.wait_ge(s_wlo, B)
                if m == TILES - 1:
                    pe.wait_ge(s_route, 2 * ROUTE_STEPS)
                    turn_weights(EARLY, 4, yt_bank)
                    pe.wait_ge(s_weight_sb, 3)
                    pe.wait_ge(s_xlo, B)

            walk_tiles(pe, layer1, spread_weights, layer2, turn_y, LAG + 1, beside)


def kernel(**inputs):
    import numpy as np
    import concourse.bacc as bacc
    from concourse.bass_utils import run_bass_kernel_spmd

    f = {name: np.asarray(a) for name, a in inputs.items()}
    x, ctx, mask = f["x"], f["ctx_1024"], f["mask_Bx1xSxS2_ik0"][:, 0]
    by_d = np.arange(H * DK).reshape(H, DK).T.reshape(-1)
    wq, bq = f["L0_xattn_w_q"][by_d], f["L0_xattn_b_q"][by_d]
    wk, bk = f["L0_xattn_w_k"][by_d], f["L0_xattn_b_k"][by_d]

    def all_rows(routed, shared, first):
        a = np.concatenate([routed, shared[None]], 0)
        a = np.moveaxis(a, 0, first).reshape(*([D] if first else []), ROWS)
        return np.pad(a, [(0, 0)] * (a.ndim - 1) + [(0, TILES * P - ROWS)])

    w1 = all_rows(f["L0_ffn_w1"], f["L0_ffn_sw1"], 1)
    w3 = all_rows(f["L0_ffn_w3"], f["L0_ffn_sw3"], 1)
    w2 = np.zeros((TILES * P, D), np.float32)
    w2[:ROWS] = np.concatenate([f["L0_ffn_w2"].reshape(-1, D), f["L0_ffn_sw2"]])
    bias = (TILES - 1) * P + BIAS_ROW
    w2[bias:bias + E + 1] = np.concatenate([f["L0_ffn_b2"], f["L0_ffn_sb2"][None]])
    w2 = w2.reshape(TILES, P, D).transpose(1, 0, 2).reshape(P, TILES * D)
    is_bias = np.zeros(TILES * P, np.float32)
    is_bias[bias:bias + E + 1] = 1
    ecols = np.stack([all_rows(f["L0_ffn_b1"], f["L0_ffn_sb1"], 0), all_rows(f["L0_ffn_b3"], f["L0_ffn_sb3"], 0),
                      is_bias])
    spread = np.zeros((E + 1, TILES * P), np.float32)
    for e in range(E + 1):
        spread[e, e * HID:(e + 1) * HID] = 1
        spread[e, bias + e] = 1

    def everywhere(*rows):
        return np.broadcast_to(np.concatenate(rows)[None], (P, sum(map(len, rows))))

    arrays = {
        "xc": np.concatenate([x, ctx.transpose(0, 2, 1)], 2),
        "mk": np.concatenate([mask, mask.transpose(0, 2, 1)], 2),
        "wqkvo": np.concatenate([wq.T, wk.T, f["L0_xattn_w_v"].T, f["L0_xattn_w_out"].T], 1),
        "cols": np.concatenate([np.stack([bq, bk, f["L0_xattn_b_v"]], 1), everywhere(f["g_xattn"], f["g_ffn"])], 1),
        "rows": everywhere(f["L0_xattn_b_out"], f["L0_ffn_gate_b"], np.arange(E, 0, -1, dtype=np.float32)),
        "gate_w": f["L0_ffn_gate_w"].T,
        "ident": np.eye(P, dtype=np.float32),
        "spread": np.pad(np.concatenate([spread] * PARTS), [(0, P - PARTS * (E + 1)), (0, 0)]),
        "experts": np.stack([w1, w3, w2], 1),
        "expert_cols": ecols.reshape(3, TILES, P).transpose(2, 0, 1),
    }
    arrays = {name: np.ascontiguousarray(a) for name, a in arrays.items()}
    nc = bacc.Bacc("TRN2", target_bir_lowering=False, num_devices=1)
    aps = {name: nc.dram_tensor(name, a.shape, mybir.dt.from_np(a.dtype), kind="ExternalInput").ap()
           for name, a in arrays.items()}
    out = nc.dram_tensor("out", (B * P, D), F32, kind="ExternalOutput").ap()
    build(nc, out=out, **aps)
    r = run_bass_kernel_spmd(nc, [arrays], core_ids=[0])
    return r.results[0]["out"].reshape(B, P, D)
```

```python
from contextlib import ExitStack

import concourse.bass as bass
from concourse import mybir

F32 = mybir.dt.float32
F32R = mybir.dt.float32r
BF16 = mybir.dt.bfloat16
I32 = mybir.dt.int32
ALU = mybir.AluOpType
ACT = mybir.ActivationFunctionType
AX = mybir.AxisListType

P = 128
B = 16
D = 128
H = 16
DK = D // H
E = 8
HID = 176
ROWS = (E + 1) * HID
TILES = -(-ROWS // P)
BIAS_ROW = 64
CHUNK = 512
CHUNKS = B * P // CHUNK
G = 4
TERMS = 6 * DK
C_ROW = 96
PARTS = 3
RING = 4
WSLICE = TILES * P // B
SHARED_TILE = E * HID // P
assert SHARED_TILE * P == E * HID and SHARED_TILE == TILES - 2
WEIGHT_RING = 4
POOL_TILES = TILES - 2
LAG = 4
EARLY = 12
EPS = 1e-5
MASKED = -(2.0 ** 60)
QSCALE = float(DK) ** -0.5
BF16_ONES = 1.0 + 0x3F80 / 2.0 ** 23


def build(nc, xc, mk, wqkvo, cols, rows, gate_w, ident, experts, expert_cols, out):
    scratch = nc.dram_tensor("parts_scratch", (RING, 10 * DK, H * P), BF16, kind="Internal").ap()

    routing = nc.dram_tensor("routing_scratch", (E, B * P), F32, kind="Internal").ap()

    with ExitStack() as ctx:
        def sb(name, shape, dt=F32):
            return ctx.enter_context(nc.sbuf_tensor(name, shape, dt))

        def sem(name):
            return ctx.enter_context(nc.semaphore(name))

        def sems(name, n):
            return [sem(f"{name}{k}") for k in range(n)]

        bank = [ctx.enter_context(nc.psum_tensor(f"bank{k}", [P, 512], F32)) for k in range(8)]
        score_bank, prob_bank = bank[0:2], bank[2:4]
        value_bank, turn_bank, in_bank, out_bank = bank[4:8]
        z1_bank, z3_bank, y_bank, yt_bank = [*bank[0:2], value_bank], [*bank[2:4], in_bank], bank[5], bank[7]

        w_sb = sb("w_sb", [P, 4 * D])
        cols_sb = sb("cols_sb", [P, 5])
        rows_sb = sb("rows_sb", [P, D + 2 * E])
        gate_sb = sb("gate_sb", [P, E])
        ident_sb = sb("ident_sb", [P, P])
        ident_bf = sb("ident_bf", [P, P], BF16)
        we_in = sb("we_in", [P, 2, 3, WSLICE])
        we_hi = sb("we_hi", [P, 3, TILES * P], F32R)
        we_lo = sb("we_lo", [P, 3, TILES * P], F32R)
        ecols_sb = sb("ecols_sb", [P, 3, TILES])
        tanh_g = sb("tanh_g", [P, 2])
        bq_scaled = sb("bq_scaled", [P, 1])
        bo_gated = sb("bo_gated", [P, D])
        half = sb("half", [P, 1])
        unused = sb("unused", [P, 1])
        xin = sb("xin", [P, RING, 2 * D])
        mask_in = sb("mask_in", [P, RING, 2 * P], I32)
        mask_add = sb("mask_add", [P, RING, 2 * P], BF16)
        stack = sb("stack", [P, RING, 2, H, P], BF16)
        v_one = sb("v_one", [P, RING, H, 32])
        x_bias = sb("x_bias", [P, RING, D])
        bn1 = sb("bn1", [P, 6])
        mv1 = sb("mv1", [P, 2, 2])
        var1 = sb("var1", [P, 1])
        rstd1 = sb("rstd1", [P, 2])
        shift1 = sb("shift1", [P, 2])
        xn = sb("xn", [P, 2, D])
        xn_t = sb("xn_t", [P, P])
        qk = sb("qk", [P, 2 * P])
        qk_rest = sb("qk_rest", [P, 2 * P])
        qk_parts = sb("qk_parts", [P, 2, 2 * PARTS, P], BF16)
        neg_max = sb("neg_max", [P, 2, H])
        max_rest = sb("max_rest", [P, H])
        max_parts = sb("max_parts", [P, PARTS * H], BF16)
        max_t = sb("max_t", [PARTS * H, 2, P], BF16)
        probs = sb("probs", [P, 4, G * P])
        values = sb("values", [P, G * P])
        recip = sb("recip", [P, H])
        attn = sb("attn", [P, D])
        attn_t = sb("attn_t", [P, P])
        x1 = sb("x1", [P, B, D])
        bn2 = sb("bn2", [P, 6])
        mv2 = sb("mv2", [P, 2])
        var2 = sb("var2", [P, 1])
        rstd2 = sb("rstd2", [P, 1])
        xn2 = sb("xn2", [P, D])
        xn2_t = sb("xn2_t", [P, P])
        x_hi = sb("x_hi", [P, B * P], F32R)
        x_lo = sb("x_lo", [P, B * P], F32R)
        logits = sb("logits", [P, B, E])
        r_max = sb("r_max", [P, B])
        r_sum = sb("r_sum", [P, B])
        r_a = sb("r_a", [P, B, E])
        r_score = sb("r_score", [P, B, E])
        r_bias = sb("r_bias", [P, B, E])
        r_pick = sb("r_pick", [P, B, E])
        r_sel = sb("r_sel", [P, 2, B, E])
        weight = sb("weight", [P, B, E])
        weight_rest = sb("weight_rest", [P, B, E])
        weight_parts = sb("weight_parts", [P, B, PARTS, E], BF16)
        weight_t = sb("weight_t", [E, CHUNK])
        weight_rows = sb("weight_rows", [P, WEIGHT_RING, CHUNK])
        last_rows = sb("last_rows", [P, CHUNK])
        z3 = sb("z3", [P, 3, CHUNK])
        z = sb("z", [P, 3, CHUNK])
        act = sb("act", [P, 3, CHUNK])
        hid = sb("hid", [P, 3, CHUNK])
        hid_hi = sb("hid_hi", [P, 5, CHUNK], F32R)
        hid_lo = sb("hid_lo", [P, 5, CHUNK], F32R)
        y_t = sb("y_t", [P, CHUNK])

        s_first = sem("s_first")
        s_const = sem("s_const")
        s_experts = sems("s_experts", 2)
        s_pad_q = sem("s_pad_q")
        s_pad_k = sem("s_pad_k")
        s_pad_v = sem("s_pad_v")
        s_half = sem("s_half")
        s_ident = sem("s_ident")
        s_tanh = sem("s_tanh")
        s_bq = sem("s_bq")
        s_bo = sem("s_bo")
        s_loaded = sems("s_loaded", RING)
        s_bn1 = sem("s_bn1")
        s_stat1 = sem("s_stat1")
        s_var1 = sem("s_var1")
        s_rstd1 = sem("s_rstd1")
        s_shift1 = sem("s_shift1")
        s_xn = sem("s_xn")
        s_mask = sem("s_mask")
        s_xbias = sem("s_xbias")
        s_xn_t = sem("s_xn_t")
        s_xn_t_sb = sem("s_xn_t_sb")
        s_qkv = sem("s_qkv")
        s_qk_sb = sem("s_qk_sb")
        s_v_sb = sem("s_v_sb")
        s_part1 = sem("s_part1")
        s_rest1 = sem("s_rest1")
        s_part2 = sem("s_part2")
        s_parts = sem("s_parts")
        s_scratch = sems("s_scratch", 2)
        s_stack = sems("s_stack", RING)
        s_score = sem("s_score")
        s_max = sem("s_max")
        s_c1 = sem("s_c1")
        s_crest = sem("s_crest")
        s_c2 = sem("s_c2")
        s_c = sem("s_c")
        s_c_t = sem("s_c_t")
        s_c_t_sb = sem("s_c_t_sb")
        s_c_row = sems("s_c_row", RING)
        s_shifted = sem("s_shifted")
        s_exp = sem("s_exp")
        s_value = sem("s_value")
        s_value_sb = sem("s_value_sb")
        s_value_t = sem("s_value_t")
        s_recip = sem("s_recip")
        s_attn = sem("s_attn")
        s_attn_t = sem("s_attn_t")
        s_attn_t_sb = sem("s_attn_t_sb")
        s_proj = sem("s_proj")
        s_x1 = sem("s_x1")
        s_bn2 = sem("s_bn2")
        s_stat2 = sem("s_stat2")
        s_var2 = sem("s_var2")
        s_rstd2 = sem("s_rstd2")
        s_xn2 = sem("s_xn2")
        s_xn2_t = sem("s_xn2_t")
        s_xn2_t_sb = sem("s_xn2_t_sb")
        s_xhi = sem("s_xhi")
        s_xlo = sem("s_xlo")
        s_logit = sem("s_logit")
        s_logit_sb = sem("s_logit_sb")
        s_whi = sem("s_whi")
        s_wlo = sem("s_wlo")
        s_route = sem("s_route")
        s_route_exp = sem("s_route_exp")
        s_weight_t = sem("s_weight_t")
        s_weight_sb = sem("s_weight_sb")
        s_weight_dram = sem("s_weight_dram")
        s_rows = sems("s_rows", WEIGHT_RING)
        s_ones = sem("s_ones")
        s_last_rows = sem("s_last_rows")
        s_z1 = sem("s_z1")
        s_z3 = sem("s_z3")
        s_z3_sb = sem("s_z3_sb")
        s_z = sem("s_z")
        s_act = sem("s_act")
        s_hid = sem("s_hid")
        s_hid_hi = sem("s_hid_hi")
        s_hid_lo = sem("s_hid_lo")
        s_last_lo = sem("s_last_lo")
        s_layer2 = sem("s_layer2")
        s_apart = sem("s_apart")
        s_y_sb = sem("s_y_sb")
        s_y_t = sem("s_y_t")
        s_result = sem("s_result")
        s_out = sem("s_out")

        N_FIRST, N_CONST = 16 * 3, 16 * 3

        ROUTE_STEPS = 23

        TURN_AT = 8, 10, TILES - 1

        def number(b):
            return 4 * b[0] + b[1]

        def place(b, n=RING):
            return b[1] % n

        def used(b, n=RING):
            return b[0] * (4 // n) + b[1] // n

        def after(b, n):
            return (b[0], b[1] + n)

        def exists(b):
            return not isinstance(b[0], int) or number(b) >= 0

        def need(eng, s, value):
            if not isinstance(value, int) or value > 0:
                eng.wait_ge(s, value)

        def apart(eng):
            eng.sem_inc(s_apart, 1)

        def weight_slice(b):
            return bass.ds(number(b) * WSLICE, WSLICE)

        def twin(m):
            return m % 2 if m < TILES - 1 else 2

        def deep(m):
            return m % 4 if m < TILES - 1 else 4

        def spans(m):
            for expert in range(m * P // HID, -(-(m + 1) * P // HID)):
                yield expert, max(expert * HID - m * P, 0), min((expert + 1) * HID - m * P, P)

        def row_dmas(c, m):
            def count(tiles):
                return sum(len(list(spans(t))) for t in tiles if t % WEIGHT_RING == m % WEIGHT_RING)
            return count(range(SHARED_TILE)) * c + count(range(m + 1))

        def pool_tiles(c, m):
            return POOL_TILES * c + min(m, POOL_TILES)

        def before(c, m, where):
            back = next(d for d in range(1, 2 * TILES) if d == 5 or where((m - d) % TILES) == where(m))
            return TILES * c + m - back + 1

        def walk_tiles(eng, beside, stage, *later, behind=None, finish=None, finish_at=0):
            def step(c, m, c_before):
                if m < TILES:
                    stage(c, m)
                if c_before is None:
                    beside(m)
                for part, lag in later:
                    if m - lag < TILES:
                        if m >= lag:
                            part(c, m - lag)
                        elif c_before is not None:
                            part(c_before, m - lag + TILES)
                if behind is not None and c_before is None:
                    behind(m)
                if finish is not None:
                    if m == TILES + finish_at:
                        finish(c)
                    elif m == finish_at and c_before is not None:
                        finish(c_before)

            for m in range(TILES):
                step(0, m, None)
            with eng.Fori(0, CHUNKS - 1) as c:
                for m in range(TILES):
                    step(c + 1, m, c)
            for m in range(TILES, TILES + LAG + 3):
                step(CHUNKS - 1, m, CHUNKS - 2)

        block = ctx.enter_context(nc.Block())

        @block.sync
        def _(sp):
            def load(b):
                need(sp, s_xbias, number(b) - RING + 1)
                need(sp, s_mask, number(b) - RING + 1)
                need(sp, s_qkv, number(b) - RING + 1)
                sp.dma_start(xin[:, place(b), :], xc[number(b)]).then_inc(s_loaded[place(b)], 16)
                sp.dma_start(mask_in[:, place(b), :], mk[number(b)]).then_inc(s_loaded[place(b)], 16)

            def store_parts(b):
                sp.wait_ge(s_parts, number(b) + 1)
                apart(sp)
                need(sp, s_stack[place(b)], 48 * used(b))
                sp.dma_start(scratch[place(b), 0:2 * PARTS * DK].rearrange("(n d) (h t) -> (d h) n t", d=DK, h=H),
                             qk_parts[:, place(b, 2)]).then_inc(s_scratch[place(b, 2)], 16)

            def fill_stacks(b):
                sp.wait_ge(s_scratch[place(b, 2)], 16 * used(b, 2) + 16)
                row = 0
                for n in (3, 2, 1):
                    apart_qk = (2 * PARTS - n) * DK
                    src = scratch[place(b), 0:2 * apart_qk].rearrange("(w r) x -> r w x", w=2)[0:n * DK]
                    sp.dma_start(stack[row:row + n * DK, place(b)].rearrange("r w h t -> r w (h t)"), src)\
                        .then_inc(s_stack[place(b)], 16)
                    row += n * DK

            def fill_max_rows(b):
                sp.wait_ge(s_c_t_sb, number(b) + 1)
                sp.dma_start(stack[C_ROW:C_ROW + PARTS, place(b), 0], max_t[:, place(b, 2), :])\
                    .then_inc(s_c_row[place(b)], 16)

            def load_weights(b):
                need(sp, s_wlo, number(b) - 1)
                apart(sp)
                c = bass.ds(number(b) * WSLICE, WSLICE)
                sp.dma_start(we_in[:, place(b, 2)], experts[:, :, c]).then_inc(s_experts[place(b, 2)], 16)

            load((0, 0))
            for dst, src in (ident_sb, ident), (cols_sb, cols), (w_sb, wqkvo):
                sp.dma_start(dst[:], src).then_inc(s_first, 16)
            load((0, 1))
            for dst, src in (rows_sb, rows), (gate_sb, gate_w), (ecols_sb, expert_cols):
                sp.dma_start(dst[:], src).then_inc(s_const, 16)
            load((0, 2))
            load((0, 3))
            load_weights((0, 0))

            def padded(n):
                sp.wait_ge(s_pad_q, 2 * n)
                sp.wait_ge(s_pad_k, 3 * n)

            store_parts((0, 0))
            padded(1)
            fill_stacks((0, 0))
            store_parts((0, 1))
            padded(2)
            store_parts((0, 2))
            fill_stacks((0, 1))
            fill_max_rows((0, 0))
            padded(RING)

            def step(s, nxt=True, new=True, stack2=True, more=True):
                if more:
                    load(after(s, 4))
                if stack2:
                    fill_stacks(after(s, 2))
                load_weights(after(s, 1))
                if nxt:
                    fill_max_rows(after(s, 1))
                if new:
                    store_parts(after(s, 3))

            with sp.Fori(0, 3) as i:
                for j in range(4):
                    step((i, j))
            step((3, 0), more=False)
            step((3, 1), more=False, new=False)
            step((3, 2), more=False, new=False, stack2=False)

            def fill_rows(c, m):
                last = m - WEIGHT_RING
                if last < 0:
                    last = max(t for t in range(SHARED_TILE) if (t - m) % WEIGHT_RING == 0) - TILES
                need(sp, s_hid, TILES * c + last + 1)
                apart(sp)
                k = m % WEIGHT_RING
                for expert, a, b in spans(m):
                    src = routing[expert:expert + 1, bass.ds(c * CHUNK, CHUNK)].broadcast_to([b - a, CHUNK])
                    sp.dma_start(weight_rows[a:b, k, :], src).then_inc(s_rows[k], 16)

            def fill_last_rows(c):
                need(sp, s_hid, TILES * c)
                apart(sp)
                sp.dma_start(last_rows[BIAS_ROW:BIAS_ROW + E, :], routing[:, bass.ds(c * CHUNK, CHUNK)])\
                    .then_inc(s_last_rows, 16)

            def store_result(c):
                sp.wait_ge(s_result, c + 1)
                apart(sp)
                sp.dma_start(out.rearrange("(n p) d -> p n d", p=P)[:, bass.ds(4 * c, 4), :],
                             x1[:, bass.ds(4 * c, 4), :]).then_inc(s_out, 16)

            def chunk_weights(c, c_before):
                sp.wait_ge(s_weight_dram, 16 * c + 16)
                for m in range(SHARED_TILE):
                    fill_rows(c, m)
                    if m == WEIGHT_RING:
                        fill_last_rows(c)
                    if m == WEIGHT_RING + 5 and c_before is not None:
                        store_result(c_before)

            sp.wait_ge(s_ones, 1)
            chunk_weights(0, None)
            with sp.Fori(0, CHUNKS - 1) as c:
                chunk_weights(c + 1, c)
            store_result(CHUNKS - 1)
            sp.wait_ge(s_out, 16 * CHUNKS)

        @block.gpsimd
        def _(pool):
            def pad_k(n, parts=range(3)):
                for m in parts:
                    a, b, value = ((32, 64, 0.0), (64, 96, 0.0), (96, 128, BF16_ONES))[m]
                    pool.memset(stack[a:b, n, 1].rearrange("p h t -> p (h t)").bitcast(F32), value).then_inc(s_pad_k, 1)
                    pool.wait_ge(s_pad_k, 3 * n + m + 1)

            pool.memset(half[:], -0.5).then_inc(s_half, 1)
            pool.memset(v_one[:], 0.0).then_inc(s_pad_v, 1)
            pool.wait_ge(s_pad_v, 1)
            pool.memset(v_one[:, :, :, DK:DK + 1], 1.0).then_inc(s_pad_v, 1)
            pool.wait_ge(s_half, 1)

            def scale1(b):
                pool.wait_ge(s_stat1, number(b) + 1)
                apart(pool)
                pool.tensor_scalar(var1[:], mv1[:, place(b, 2), 1:2], EPS, None, ALU.add).then_inc(s_var1, 1)
                pool.wait_ge(s_var1, number(b) + 1)
                need(pool, s_xn, number(b) - 1)
                k = slice(place(b, 2), place(b, 2) + 1)
                apart(pool)
                pool.tensor_tensor(rstd1[:, k], var1[:], half[:], ALU.pow).then_inc(s_rstd1, 1)
                pool.wait_ge(s_rstd1, number(b) + 1)
                apart(pool)
                pool.tensor_scalar(shift1[:, k], mv1[:, place(b, 2), 0:1], rstd1[:, k], -1.0,
                                   ALU.mult, ALU.mult).then_inc(s_shift1, 1)

            def bias_x(b):
                need(pool, s_x1, number(b) - RING + 1)
                pool.tensor_tensor(x_bias[:, place(b), :], xin[:, place(b), 0:D], bo_gated[:], ALU.add)\
                    .then_inc(s_xbias, 1)

            def cut_max(b):
                pool.wait_ge(s_max, 4 * number(b) + 4)
                need(pool, s_c_t, number(b))
                m = neg_max[:, place(b, 2), :]
                apart(pool)
                pool.tensor_copy(max_parts[:, 0:H], m).then_inc(s_c1, 1)
                pool.wait_ge(s_c1, number(b) + 1)
                pool.tensor_tensor(max_rest[:], m, max_parts[:, 0:H], ALU.subtract).then_inc(s_crest, 1)
                pool.wait_ge(s_crest, number(b) + 1)
                apart(pool)
                pool.tensor_copy(max_parts[:, H:2 * H], max_rest[:]).then_inc(s_c2, 1)
                pool.wait_ge(s_c2, number(b) + 1)
                pool.tensor_tensor(max_parts[:, 2 * H:3 * H], max_rest[:], max_parts[:, H:2 * H], ALU.subtract)\
                    .then_inc(s_c, 1)

            def scale2(b):
                pool.wait_ge(s_stat2, number(b) + 1)
                need(pool, s_xn2, number(b))
                apart(pool)
                pool.tensor_scalar(var2[:], mv2[:, 1:2], EPS, None, ALU.add).then_inc(s_var2, 1)
                pool.wait_ge(s_var2, number(b) + 1)
                pool.tensor_tensor(rstd2[:], var2[:], half[:], ALU.pow).then_inc(s_rstd2, 1)

            def weights_lo(b):
                pool.wait_ge(s_whi, number(b) + 1)
                c = weight_slice(b)
                pool.tensor_tensor(we_lo[:, :, c], we_in[:, place(b, 2)], we_hi[:, :, c], ALU.subtract)\
                    .then_inc(s_wlo, 1)

            def x_lo_part(b):
                pool.wait_ge(s_xhi, number(b) + 1)
                c = bass.ds(number(b) * P, P)
                pool.tensor_tensor(x_lo[:, c], xn2_t[:], x_hi[:, c], ALU.subtract).then_inc(s_xlo, 1)

            scale1((0, 0))
            pool.wait_ge(s_first, N_FIRST)
            pool.tensor_scalar(bq_scaled[:], cols_sb[:, 0:1], QSCALE, None, ALU.mult).then_inc(s_bq, 1)
            pool.wait_ge(s_bq, 1)
            pad_k(0)
            scale1((0, 1))
            pool.tensor_copy(ident_bf[:], ident_sb[:]).then_inc(s_ident, 1)
            scale1((0, 2))
            pool.wait_ge(s_shift1, 3)
            pad_k(1)
            pad_k(2)
            pool.wait_ge(s_tanh, 1)
            pool.wait_ge(s_const, N_CONST)
            pool.tensor_scalar(bo_gated[:], rows_sb[:, 0:D], tanh_g[:, 0:1], None, ALU.mult).then_inc(s_bo, 1)
            pool.wait_ge(s_bo, 1)
            for j in range(3):
                bias_x((0, j))
            pool.wait_ge(s_xbias, 3)
            pad_k(3, [0])
            cut_max((0, 0))
            scale1((0, 3))
            pool.wait_ge(s_shift1, 4)
            pad_k(3, [1, 2])

            def step(s, prev=True, nxt=True, new=True):
                if new and prev:
                    scale1(after(s, 3))
                if nxt:
                    cut_max(after(s, 1))
                if prev:
                    scale2(after(s, -1))
                if new:
                    bias_x(after(s, 3))
                weights_lo(s)
                if prev:
                    x_lo_part(after(s, -1))

            step((0, 0), prev=False)
            with pool.Fori(0, 3) as i:
                for j in range(1, 5):
                    step((i, j))
            step((3, 1), new=False)
            step((3, 2), new=False)
            step((3, 3), new=False, nxt=False)

            def cut_hidden(c, m):
                n = TILES * c + m
                if m >= POOL_TILES:
                    return
                pool.wait_ge(s_hid_hi, n + 1)
                need(pool, s_layer2, before(c, m, deep))
                pool.tensor_tensor(hid_lo[:, deep(m)], hid[:, twin(m)], hid_hi[:, deep(m)], ALU.subtract)\
                    .then_inc(s_hid_lo, 1)

            def beside(m):
                if m == 0:
                    scale2((3, 3))
                if m == 4:
                    x_lo_part((3, 3))

            walk_tiles(pool, beside, cut_hidden)

        @block.scalar
        def _(act_e):
            def normalise(b):
                act_e.wait_ge(s_shift1, number(b) + 1)
                need(act_e, s_xn_t, number(b) - 1)
                k = slice(place(b, 2), place(b, 2) + 1)
                act_e.activation(xn[:, place(b, 2), :], xin[:, place(b), 0:D], ACT.Identity, bias=shift1[:, k],
                                 scale=rstd1[:, k]).then_inc(s_xn, 1)

            def weights_hi(b):
                act_e.wait_ge(s_experts[place(b, 2)], 16 * used(b, 2) + 16)
                act_e.activation(we_hi[:, :, weight_slice(b)], we_in[:, place(b, 2)], ACT.Copy).then_inc(s_whi, 1)

            def copy_xn_t(b):
                act_e.wait_ge(s_xn_t, number(b) + 1)
                need(act_e, s_qkv, number(b))
                act_e.activation(xn_t[:], in_bank[:, 384:512], ACT.Copy).then_inc(s_xn_t_sb, 1)

            def copy_qk(b):
                act_e.wait_ge(s_qkv, number(b) + 1)
                need(act_e, s_rest1, number(b))
                act_e.activation(qk[:, 0:P], in_bank[:, 0:P], ACT.Identity, bias=bq_scaled[:, 0:1],
                                 scale=QSCALE).then_inc(s_qk_sb, 1)
                act_e.activation(qk[:, P:2 * P], in_bank[:, P:2 * P], ACT.Identity, bias=cols_sb[:, 1:2])\
                    .then_inc(s_qk_sb, 1)

            def copy_v(b):
                need(act_e, s_value, 4 * number(b) - 4 * (RING - 1))
                act_e.activation(v_one[:, place(b), :, 0:DK],
                                 in_bank[:, 256:384].rearrange("p (h d) -> p h d", d=DK), ACT.Copy)\
                    .then_inc(s_v_sb, 1)

            def copy_max_t(b):
                act_e.wait_ge(s_c_t, number(b) + 1)
                o = after(b, -2)
                if exists(o):
                    act_e.wait_ge(s_c_row[place(o)], 16 * used(o) + 16)
                act_e.activation(max_t[:, place(b, 2), :], turn_bank[0:PARTS * H, 0:P // 2].bitcast(BF16), ACT.Copy)\
                    .then_inc(s_c_t_sb, 1)

            def exp(b, g):
                act_e.wait_ge(s_shifted, 4 * number(b) + g + 1)
                need(act_e, s_value, 4 * number(b) + g - 3)
                act_e.activation(probs[:, g, :], prob_bank[g % 2][:, :], ACT.Exp).then_inc(s_exp, 1)

            def copy_values(b):
                act_e.wait_ge(s_value, 4 * number(b) + 4)
                need(act_e, s_value_t, number(b))
                act_e.activation(values[:], value_bank[:, :], ACT.Copy).then_inc(s_value_sb, 1)

            def copy_attn_t(b):
                act_e.wait_ge(s_attn_t, number(b) + 1)
                need(act_e, s_proj, number(b))
                act_e.activation(attn_t[:], out_bank[:, 0:P], ACT.Identity, bias=cols_sb[:, 2:3])\
                    .then_inc(s_attn_t_sb, 1)

            def copy_xn2_t(b):
                act_e.wait_ge(s_xn2_t, number(b) + 1)
                need(act_e, s_logit, number(b))
                need(act_e, s_xlo, number(b))
                act_e.activation(xn2_t[:], out_bank[:, 0:P], ACT.Copy).then_inc(s_xn2_t_sb, 1)
                act_e.activation(x_hi[:, bass.ds(number(b) * P, P)], out_bank[:, 0:P], ACT.Copy).then_inc(s_xhi, 1)

            def copy_logits(b):
                act_e.wait_ge(s_logit, number(b) + 1)
                act_e.activation(logits[:, bass.ds(number(b), 1), :].rearrange("p n e -> p (n e)"),
                                 out_bank[:, 0:E], ACT.Copy).then_inc(s_logit_sb, 1)

            normalise((0, 0))
            copy_xn_t((0, 0))
            act_e.wait_ge(s_bq, 1)
            copy_qk((0, 0))
            act_e.wait_ge(s_pad_v, 2)
            copy_v((0, 0))
            act_e.activation(tanh_g[:], cols_sb[:, 3:5], ACT.Tanh).then_inc(s_tanh, 1)
            act_e.wait_ge(s_half, 1)
            normalise((0, 1))
            copy_xn_t((0, 1))
            copy_qk((0, 1))
            copy_v((0, 1))
            normalise((0, 2))
            copy_xn_t((0, 2))
            copy_qk((0, 2))
            copy_v((0, 2))
            copy_max_t((0, 0))

            def route_exp(group):
                n = slice(0, EARLY) if group == 0 else slice(EARLY, B)
                act_e.wait_ge(s_route, ROUTE_STEPS * group + 2)
                act_e.activation(r_a[:, n], r_a[:, n], ACT.Exp).then_inc(s_route_exp, 1)

            def copy_weights(c, turned):
                act_e.wait_ge(s_weight_t, c + 1)
                if c:
                    act_e.wait_ge(s_weight_dram, 16 * c)
                act_e.activation(weight_t[:], turned[0:E, :], ACT.Copy).then_inc(s_weight_sb, 1)
                act_e.wait_ge(s_weight_sb, c + 1)
                act_e.dma_start(routing[:, c * CHUNK:(c + 1) * CHUNK], weight_t[:]).then_inc(s_weight_dram, 16)

            def step(s, prev=True, nxt=True, new=True, route=False):
                weights_hi(s)
                if new:
                    normalise(after(s, 3))
                if prev:
                    copy_attn_t(after(s, -1))
                if new:
                    copy_xn_t(after(s, 3))
                exp(s, 0)
                exp(s, 1)
                if route:
                    route_exp(0)
                if new:
                    copy_qk(after(s, 3))
                    copy_v(after(s, 3))
                exp(s, 2)
                exp(s, 3)
                if nxt:
                    copy_max_t(after(s, 1))
                if prev:
                    copy_xn2_t(after(s, -1))
                copy_values(s)
                if prev:
                    copy_logits(after(s, -1))

            step((0, 0), prev=False)
            with act_e.Fori(0, 3) as i:
                for j in range(1, 5):
                    step((i, j))
            step((3, 1), new=False, route=True)
            step((3, 2), new=False)
            weights_hi((3, 3))
            exp((3, 3), 0)
            exp((3, 3), 1)
            copy_attn_t((3, 2))
            exp((3, 3), 2)
            exp((3, 3), 3)
            act_e.activation(unused[:], half[:], ACT.Silu)
            copy_weights(0, in_bank)
            copy_values((3, 3))
            act_e.wait_ge(s_const, N_CONST)

            def copy_z3(c, m):
                act_e.wait_ge(s_z3, TILES * c + m + 1)
                need(act_e, s_z, before(c, m, twin))
                act_e.activation(z3[:, twin(m)], z3_bank[twin(m)][:, :], ACT.Identity,
                                 bias=ecols_sb[:, 1, m:m + 1]).then_inc(s_z3_sb, 1)

            def silu(c, m):
                act_e.wait_ge(s_z, TILES * c + m + 1)
                need(act_e, s_hid, before(c, m, twin))
                act_e.activation(act[:, twin(m)], z[:, twin(m)], ACT.Silu).then_inc(s_act, 1)

            def cut_hi(c, m):
                act_e.wait_ge(s_hid, TILES * c + m + 1)
                need(act_e, s_layer2, before(c, m, deep))
                act_e.activation(hid_hi[:, deep(m)], hid[:, twin(m)], ACT.Copy).then_inc(s_hid_hi, 1)

            def copy_y(c):
                act_e.wait_ge(s_layer2, TILES * c + TILES)
                act_e.activation(y_t[:], y_bank[:, :], ACT.Copy, scale=tanh_g[:, 1:2]).then_inc(s_y_sb, 1)

            def beside(m):
                if m == 0:
                    copy_xn2_t((3, 2))
                if m == 1:
                    copy_logits((3, 2))
                    copy_attn_t((3, 3))
                if m == 4:
                    copy_xn2_t((3, 3))
                if m == 5:
                    copy_logits((3, 3))

            def behind(m):
                if m == 6:
                    route_exp(1)
                if m in TURN_AT:
                    copy_weights(TURN_AT.index(m) + 1, yt_bank)

            walk_tiles(act_e, beside, copy_z3, (silu, 1), (cut_hi, 2), behind=behind, finish=copy_y,
                       finish_at=LAG - 1)

        @block.vector
        def _(dve):
            def stats1(b):
                dve.wait_ge(s_loaded[place(b)], 32 * used(b) + 32)
                need(dve, s_stat1, number(b))
                dve.bn_stats(bn1[:], xin[:, place(b), 0:D]).then_inc(s_bn1, 1)
                dve.wait_ge(s_bn1, number(b) + 1)
                need(dve, s_shift1, number(b) - 1)
                apart(dve)
                dve.bn_aggr(mv1[:, place(b, 2), :], bn1[:]).then_inc(s_stat1, 1)

            def add_of_mask(b):
                dve.wait_ge(s_loaded[place(b)], 32 * used(b) + 32)
                need(dve, s_shifted, 4 * number(b) - 4 * (RING - 1))
                apart(dve)
                dve.tensor_scalar(mask_add[:, place(b), :], mask_in[:, place(b), :], 0.0, MASKED,
                                  ALU.is_equal, ALU.mult).then_inc(s_mask, 1)

            def part(b, i):
                return qk_parts[:, place(b, 2), i:2 * PARTS - i:2 * PARTS - 1 - 2 * i]

            qk_pair = qk[:].rearrange("p (w t) -> p w t", w=2)
            rest_pair = qk_rest[:].rearrange("p (w t) -> p w t", w=2)

            def cut1(b):
                dve.wait_ge(s_qk_sb, 2 * number(b) + 2)
                need(dve, s_scratch[place(b, 2)], 16 * used(b, 2))
                dve.tensor_copy(part(b, 0), qk_pair).then_inc(s_part1, 1)

            def cut2(b):
                dve.wait_ge(s_part1, number(b) + 1)
                dve.tensor_tensor(rest_pair, qk_pair, part(b, 0), ALU.subtract).then_inc(s_rest1, 1)

            def cut3(b):
                dve.wait_ge(s_rest1, number(b) + 1)
                dve.tensor_copy(part(b, 1), rest_pair).then_inc(s_part2, 1)

            def cut4(b):
                dve.wait_ge(s_part2, number(b) + 1)
                dve.tensor_tensor(part(b, 2), rest_pair, part(b, 1), ALU.subtract).then_inc(s_parts, 1)

            def cut_qk(b):
                for cut in (cut1, cut2, cut3, cut4):
                    cut(b)

            def row_max(b, g):
                dve.wait_ge(s_score, 4 * number(b) + g + 1)
                if g == 0:
                    need(dve, s_c, number(b) - 1)
                dve.tensor_reduce(neg_max[:, place(b, 2), G * g:G * g + G],
                                  score_bank[g % 2][:, :].rearrange("p (h k) -> p h k", h=G), AX.X, ALU.max,
                                  negate=True).then_inc(s_max, 1)

            def divide(b):
                dve.wait_ge(s_value_t, number(b) + 1)
                t = turn_bank[:, :].rearrange("p (h c) -> p h c", c=32)
                dve.reciprocal(recip[:].rearrange("p (h c) -> p h c", c=1), t[:, :, DK:DK + 1]).then_inc(s_recip, 1)
                dve.wait_ge(s_recip, number(b) + 1)
                need(dve, s_attn_t, number(b))
                dve.tensor_tensor(attn[:].rearrange("p (h d) -> p h d", d=DK), t[:, :, 0:DK],
                                  recip[:].rearrange("p (h c) -> p h c", c=1).broadcast_to([P, H, DK]),
                                  ALU.mult).then_inc(s_attn, 1)

            def residual(b):
                dve.wait_ge(s_proj, number(b) + 1)
                dve.wait_ge(s_xbias, number(b) + 1)
                x1_b = x1[:, bass.ds(number(b), 1), :].rearrange("p n d -> p (n d)")
                dve.scalar_tensor_tensor(x1_b, out_bank[:, 0:D], tanh_g[:, 0:1], x_bias[:, place(b), :],
                                         ALU.mult, ALU.add).then_inc(s_x1, 1)
                dve.wait_ge(s_x1, number(b) + 1)
                apart(dve)
                dve.bn_stats(bn2[:], x1_b).then_inc(s_bn2, 1)

            def stats2(b):
                dve.wait_ge(s_bn2, number(b) + 1)
                need(dve, s_xn2, number(b))
                apart(dve)
                dve.bn_aggr(mv2[:], bn2[:]).then_inc(s_stat2, 1)

            def normalise2(b):
                dve.wait_ge(s_rstd2, number(b) + 1)
                need(dve, s_xn2_t, number(b))
                dve.tensor_scalar(xn2[:], x1[:, bass.ds(number(b), 1), :].rearrange("p n d -> p (n d)"),
                                  mv2[:, 0:1], rstd2[:], ALU.subtract, ALU.mult).then_inc(s_xn2, 1)

            def pad_q(n):
                for a, b in ((32, 64), (64, 128)):
                    dve.memset(stack[a:b, n, 0].rearrange("p h t -> p (h t)").bitcast(F32), 0.0).then_inc(s_pad_q, 1)

            pad_q(0)
            stats1((0, 0))
            add_of_mask((0, 0))
            pad_q(1)
            stats1((0, 1))
            pad_q(2)
            cut_qk((0, 0))
            add_of_mask((0, 1))
            stats1((0, 2))
            pad_q(3)
            cut_qk((0, 1))
            add_of_mask((0, 2))
            dve.memset(last_rows[:], 1.0).then_inc(s_ones, 1)
            cut_qk((0, 2))
            for g in range(4):
                row_max((0, 0), g)

            def route(group, first, last):
                n = slice(0, EARLY) if group == 0 else slice(EARLY, B)

                def col(t):
                    return t[:, n].rearrange("p (n c) -> p n c", c=1).broadcast_to([P, n.stop - n.start, E])

                def row(t):
                    return t.rearrange("p (n e) -> p n e", n=1).broadcast_to([P, n.stop - n.start, E])

                for k in range(first, last + 1):
                    if k == 0:
                        dve.wait_ge(s_const, N_CONST)
                        dve.wait_ge(s_logit_sb, n.stop)
                    if group or k:
                        dve.wait_ge(s_route, ROUTE_STEPS * group + k)
                    if k == 0:
                        op = dve.tensor_reduce(r_max[:, n], logits[:, n], AX.X, ALU.max)
                    elif k == 1:
                        op = dve.tensor_tensor(r_a[:, n], logits[:, n], col(r_max), ALU.subtract)
                    elif k == 2:
                        dve.wait_ge(s_route_exp, group + 1)
                        op = dve.tensor_reduce(r_sum[:, n], r_a[:, n], AX.X, ALU.add)
                    elif k == 3:
                        op = dve.reciprocal(r_sum[:, n], r_sum[:, n])
                    elif k == 4:
                        op = dve.tensor_tensor(r_score[:, n], r_a[:, n], col(r_sum), ALU.mult)
                    elif k == 5:
                        op = dve.tensor_tensor(r_bias[:, n], r_score[:, n], row(rows_sb[:, D:D + E]), ALU.add)
                    elif k in (6, 12):
                        op = dve.tensor_reduce(r_max[:, n], r_bias[:, n], AX.X, ALU.max)
                    elif k in (7, 13):
                        op = dve.tensor_tensor(r_pick[:, n], r_bias[:, n], col(r_max), ALU.is_equal)
                    elif k in (8, 14):
                        op = dve.tensor_tensor(r_pick[:, n], r_pick[:, n], row(rows_sb[:, D + E:D + 2 * E]), ALU.mult)
                    elif k in (9, 15):
                        op = dve.tensor_reduce(r_max[:, n], r_pick[:, n], AX.X, ALU.max)
                    elif k in (10, 16):
                        op = dve.tensor_tensor(r_sel[:, k // 16, n], r_pick[:, n], col(r_max), ALU.is_equal)
                    elif k == 11:
                        op = dve.scalar_tensor_tensor(r_bias[:, n], r_sel[:, 0, n], -3e38, r_bias[:, n],
                                                      ALU.mult, ALU.add)
                    elif k == 17:
                        op = dve.tensor_tensor(r_pick[:, n], r_sel[:, 0, n], r_sel[:, 1, n], ALU.add)
                    elif k == 18:
                        op = dve.tensor_tensor(weight[:, n], r_score[:, n], r_pick[:, n], ALU.mult)
                    elif k == 19:
                        op = dve.tensor_copy(weight_parts[:, n, 0], weight[:, n])
                    elif k == 20:
                        op = dve.tensor_tensor(weight_rest[:, n], weight[:, n], weight_parts[:, n, 0], ALU.subtract)
                    elif k == 21:
                        op = dve.tensor_copy(weight_parts[:, n, 1], weight_rest[:, n])
                    elif k == 22:
                        op = dve.tensor_tensor(weight_parts[:, n, 2], weight_rest[:, n], weight_parts[:, n, 1],
                                               ALU.subtract)
                    op.then_inc(s_route, 1)

            def step(s, prev=True, nxt=True, new=True, routing=False):
                p, n, w = after(s, -1), after(s, 1), after(s, 3)
                if new:
                    stats1(w)
                if nxt:
                    row_max(n, 0)
                    row_max(n, 1)
                if prev:
                    divide(p)
                if nxt:
                    row_max(n, 2)
                    row_max(n, 3)
                if new:
                    add_of_mask(w)
                if routing:
                    route(0, 0, 1)
                if prev:
                    residual(p)
                    stats2(p)
                if routing:
                    route(0, 2, 5)
                if new:
                    cut1(w)
                    cut2(w)
                if prev:
                    normalise2(p)
                if new:
                    cut3(w)
                    cut4(w)

            dve.wait_ge(s_tanh, 1)
            step((0, 0), prev=False)
            with dve.Fori(0, 3) as i:
                for j in range(1, 5):
                    step((i, j))
            step((3, 1), new=False, routing=True)
            route(0, 6, 11)
            step((3, 2), new=False)
            route(0, 12, 16)
            divide((3, 2))
            route(0, 17, 22)
            residual((3, 2))
            stats2((3, 2))
            normalise2((3, 2))

            def gate(c, m):
                n = TILES * c + m
                dve.wait_ge(s_z1, n + 1)
                dve.wait_ge(s_z3_sb, n + 1)
                need(dve, s_act, before(c, m, twin))
                dve.scalar_tensor_tensor(z[:, twin(m)], z1_bank[twin(m)][:, :], ecols_sb[:, 0, m:m + 1],
                                         z3[:, twin(m)], ALU.add, ALU.mult).then_inc(s_z, 1)

            def weigh(c, m):
                n = TILES * c + m
                dve.wait_ge(s_act, n + 1)
                if m < SHARED_TILE:
                    dve.wait_ge(s_rows[m % WEIGHT_RING], row_dmas(c, m) * 16)
                if m == TILES - 1:
                    dve.wait_ge(s_last_rows, 16 * c + 16)
                if m < TILES - 1:
                    need(dve, s_hid_lo, pool_tiles(c, max(m - 1, 0)))
                if m == SHARED_TILE:
                    dve.tensor_copy(hid[:, twin(m)], act[:, twin(m)]).then_inc(s_hid, 1)
                else:
                    rows_m = weight_rows[:, m % WEIGHT_RING] if m < SHARED_TILE else last_rows[:]
                    dve.scalar_tensor_tensor(hid[:, twin(m)], act[:, twin(m)], ecols_sb[:, 2, m:m + 1], rows_m,
                                             ALU.add, ALU.mult).then_inc(s_hid, 1)
                if isinstance(c, int) and c == 0 and 6 <= m < 10:
                    route(1, 4 * m - 18, 4 * m - 17)

            def last_lo(c, m):
                if m >= POOL_TILES:
                    dve.wait_ge(s_hid_hi, TILES * c + m + 1)
                    dve.tensor_tensor(hid_lo[:, deep(m)], hid[:, twin(m)], hid_hi[:, deep(m)], ALU.subtract)\
                        .then_inc(s_last_lo, 1)

            def finish(c):
                dve.wait_ge(s_y_t, c + 1)
                x1_c = x1[:, bass.ds(4 * c, 4), :].rearrange("p n d -> p (n d)")
                dve.tensor_tensor(x1_c, yt_bank[:, :], x1_c, ALU.add).then_inc(s_result, 1)

            def beside(m):
                if m == 0:
                    divide((3, 3))
                if m == 2:
                    residual((3, 3))
                    stats2((3, 3))
                if m == 3:
                    normalise2((3, 3))
                if m == 6:
                    route(1, 0, 1)
                if m == 7:
                    route(1, 2, 5)
                if 8 <= m < 12:
                    route(1, 4 * m - 24, 4 * m - 23 if m < 11 else ROUTE_STEPS - 1)

            walk_tiles(dve, beside, gate, (weigh, 1), (last_lo, 2), finish=finish, finish_at=LAG + 2)

        @block.tensor
        def _(pe):
            def turn_xn(b):
                pe.wait_ge(s_xn, number(b) + 1)
                need(pe, s_v_sb, number(b))
                pe.transpose(in_bank[:, 384:512], xn[:, place(b, 2), :], ident_sb[:]).then_inc(s_xn_t, 1)

            def project_in(b):
                pe.wait_ge(s_xn_t_sb, number(b) + 1)
                ctx_t = xin[:, place(b), D:2 * D]
                pe.matmul(in_bank[:, 0:P], w_sb[:, 0:D], xn_t[:], start=True, stop=True)
                pe.matmul(in_bank[:, P:2 * P], w_sb[:, D:2 * D], ctx_t, start=True, stop=True)
                pe.matmul(in_bank[:, 2 * P:3 * P], ctx_t, w_sb[:, 2 * D:3 * D], start=True, stop=True)\
                    .then_inc(s_qkv, 1)

            def scores(b, g):
                if g == 0:
                    pe.wait_ge(s_stack[place(b)], 48 * used(b) + 48)
                    pe.wait_ge(s_mask, number(b) + 1)
                need(pe, s_max, 4 * number(b) + g - 1)
                o = score_bank[g % 2]
                for n in range(G):
                    pe.matmul(o[:, n * P:(n + 1) * P], stack[0:C_ROW, place(b), 0, G * g + n, :],
                              stack[0:C_ROW, place(b), 1, G * g + n, :], start=n == 0, stop=False,
                              skip_group_check=True)
                pe.matmul(o[:, :].rearrange("p (n k) -> p n k", n=G), ident_bf[:],
                          mask_add[:, place(b), 0:P].rearrange("p (n k) -> p n k", n=1).broadcast_to([P, G, P]),
                          start=False, stop=True, skip_group_check=True).then_inc(s_score, 1)

            def shifted(b, g):
                if g == 0:
                    pe.wait_ge(s_c_row[place(b)], 16 * used(b) + 16)
                need(pe, s_exp, 4 * number(b) + g - 1)
                o = prob_bank[g % 2]
                for n in range(G):
                    pe.matmul(o[:, n * P:(n + 1) * P], stack[:, place(b), 1, G * g + n, :],
                              stack[:, place(b), 0, G * g + n, :], start=n == 0, stop=False,
                              skip_group_check=True)
                pe.matmul(o[:, :].rearrange("p (n k) -> p n k", n=G), ident_bf[:],
                          mask_add[:, place(b), P:2 * P].rearrange("p (n k) -> p n k", n=1).broadcast_to([P, G, P]),
                          start=False, stop=True, skip_group_check=True).then_inc(s_shifted, 1)

            def weigh_values(b, g):
                pe.wait_ge(s_exp, 4 * number(b) + g + 1)
                if g == 0:
                    pe.wait_ge(s_v_sb, number(b) + 1)
                    need(pe, s_value_sb, number(b))
                for n in range(G):
                    mm = pe.matmul(value_bank[32 * n:32 * n + 32, g * P:(g + 1) * P], v_one[:, place(b), G * g + n, :],
                                   probs[:, g, n * P:(n + 1) * P], start=True, stop=True)
                mm.then_inc(s_value, 1)

            def turn_values(b):
                pe.wait_ge(s_value_sb, number(b) + 1)
                pe.wait_ge(s_c_t_sb, number(b) + 2 if not isinstance(b[0], int) else min(number(b) + 2, B))
                for g in range(4):
                    t = pe.transpose(turn_bank[:, g * P:(g + 1) * P], values[:, g * P:(g + 1) * P], ident_sb[:])
                t.then_inc(s_value_t, 1)

            def turn_attn(b):
                pe.wait_ge(s_attn, number(b) + 1)
                need(pe, s_logit_sb, number(b))
                pe.transpose(out_bank[:, 0:P], attn[:], ident_sb[:]).then_inc(s_attn_t, 1)

            def project_out(b):
                pe.wait_ge(s_attn_t_sb, number(b) + 1)
                pe.matmul(out_bank[:, 0:P], attn_t[:], w_sb[:, 3 * D:4 * D], start=True, stop=True)\
                    .then_inc(s_proj, 1)

            def turn_max(b):
                pe.wait_ge(s_c, number(b) + 1)
                need(pe, s_attn, number(b) - 1)
                apart(pe)
                pe.transpose(turn_bank[0:PARTS * H, 0:P // 2].bitcast(BF16), max_parts[:], ident_bf[:]).then_inc(s_c_t, 1)

            def turn_xn2(b):
                pe.wait_ge(s_xn2, number(b) + 1)
                pe.transpose(out_bank[:, 0:P], xn2[:], ident_sb[:]).then_inc(s_xn2_t, 1)

            def route(b):
                pe.wait_ge(s_xhi, number(b) + 1)
                pe.matmul(out_bank[:, 0:E], xn2_t[:], gate_sb[:], start=True, stop=True).then_inc(s_logit, 1)

            pe.wait_ge(s_first, N_FIRST)
            turn_xn((0, 0))
            project_in((0, 0))
            turn_xn((0, 1))
            project_in((0, 1))
            turn_xn((0, 2))
            project_in((0, 2))
            pe.wait_ge(s_ident, 1)
            for g in range(4):
                scores((0, 0), g)
            turn_max((0, 0))
            pe.wait_ge(s_const, N_CONST)

            def step(s, prev=True, nxt=True, new=True, ahead=True):
                p, n, w = after(s, -1), after(s, 1), after(s, 3)
                if nxt:
                    scores(n, 2)
                    scores(n, 3)
                if prev:
                    turn_attn(p)
                shifted(s, 0)
                if new:
                    turn_xn(w)
                shifted(s, 1)
                if prev:
                    project_out(p)
                if new:
                    project_in(w)
                shifted(s, 2)
                weigh_values(s, 0)
                shifted(s, 3)
                if nxt:
                    turn_max(n)
                weigh_values(s, 1)
                weigh_values(s, 2)
                if prev:
                    turn_xn2(p)
                weigh_values(s, 3)
                if ahead:
                    scores(after(s, 2), 0)
                    scores(after(s, 2), 1)
                if prev:
                    route(p)
                turn_values(s)

            scores((0, 1), 0)
            scores((0, 1), 1)
            step((0, 0), prev=False)
            with pe.Fori(0, 3) as i:
                for j in range(1, 5):
                    step((i, j))
            step((3, 1), new=False)
            step((3, 2), new=False, ahead=False)

            def turn_weights(c, into):
                pe.wait_ge(s_route, ROUTE_STEPS * (1 if c * CHUNK // P < EARLY else 2))
                if c:
                    pe.wait_ge(s_weight_sb, c)
                    pe.wait_ge(s_logit_sb, B)
                for t in range(CHUNK // P):
                    for i in range(PARTS):
                        turned = pe.matmul(into[0:E, t * P:(t + 1) * P], weight_parts[:, c * (CHUNK // P) + t, i],
                                           ident_bf[:], start=i == 0, stop=i == PARTS - 1)
                turned.then_inc(s_weight_t, 1)

            shifted((3, 3), 0)
            shifted((3, 3), 1)
            weigh_values((3, 3), 0)
            turn_attn((3, 2))
            shifted((3, 3), 2)
            weigh_values((3, 3), 1)
            shifted((3, 3), 3)
            project_out((3, 2))
            turn_weights(0, in_bank)
            weigh_values((3, 3), 2)
            weigh_values((3, 3), 3)
            pe.wait_ge(s_wlo, 13)
            pe.wait_ge(s_xlo, EARLY)
            pe.wait_ge(s_exp, 4 * B)
            pe.wait_ge(s_v_sb, B)

            def layer1(c, m):
                cols_m = slice(m * P, (m + 1) * P)
                tok = bass.ds(c * CHUNK, CHUNK)
                k = twin(m)
                for w, o, done, read in ((1, z3_bank[k], s_z3, s_z3_sb), (0, z1_bank[k], s_z1, s_z)):
                    need(pe, read, before(c, m, twin))
                    pe.matmul(o[:, :], we_hi[:, w, cols_m], x_hi[:, tok], start=True, stop=False)
                    pe.matmul(o[:, :], we_hi[:, w, cols_m], x_lo[:, tok], start=False, stop=False)
                    pe.matmul(o[:, :], we_lo[:, w, cols_m], x_hi[:, tok], start=False, stop=True).then_inc(done, 1)

            def layer2(c, m):
                n = TILES * c + m
                cols_m = slice(m * P, (m + 1) * P)
                pe.wait_ge(s_hid_hi, n + 1)
                if m == 0:
                    need(pe, s_y_sb, c)
                pe.matmul(y_bank[:, :], we_hi[:, 2, cols_m], hid_hi[:, deep(m)], start=m == 0, stop=False)
                pe.matmul(y_bank[:, :], we_lo[:, 2, cols_m], hid_hi[:, deep(m)], start=False, stop=False)
                if m >= POOL_TILES:
                    pe.wait_ge(s_last_lo, (TILES - POOL_TILES) * c + m - POOL_TILES + 1)
                else:
                    pe.wait_ge(s_hid_lo, pool_tiles(c, m + 1))
                pe.matmul(y_bank[:, :], we_hi[:, 2, cols_m], hid_lo[:, deep(m)], start=False, stop=m == TILES - 1)\
                    .then_inc(s_layer2, 1)

            def turn_y(c):
                pe.wait_ge(s_y_sb, c + 1)
                for t in range(CHUNK // P):
                    tr = pe.transpose(yt_bank[:, t * P:(t + 1) * P], y_t[:, t * P:(t + 1) * P], ident_sb[:])
                tr.then_inc(s_y_t, 1)

            def beside(m):
                if m == 0:
                    turn_xn2((3, 2))
                    turn_values((3, 3))
                if m == 1:
                    route((3, 2))
                    turn_attn((3, 3))
                if m == 2:
                    project_out((3, 3))
                if m == 4:
                    turn_xn2((3, 3))
                if m == 5:
                    route((3, 3))
                if m == 9:
                    pe.wait_ge(s_wlo, B)
                if m == TILES - 1:
                    pe.wait_ge(s_xlo, B)

            def behind(m):
                if m in TURN_AT:
                    turn_weights(TURN_AT.index(m) + 1, yt_bank)

            walk_tiles(pe, beside, layer1, (layer2, LAG), behind=behind, finish=turn_y, finish_at=LAG + 1)


def kernel(**inputs):
    import numpy as np
    import concourse.bacc as bacc
    from concourse.bass_utils import run_bass_kernel_spmd

    f = {name: np.asarray(a) for name, a in inputs.items()}
    x, ctx, mask = f["x"], f["ctx_1024"], f["mask_Bx1xSxS2_ik0"][:, 0]
    by_d = np.arange(H * DK).reshape(H, DK).T.reshape(-1)
    wq, bq = f["L0_xattn_w_q"][by_d], f["L0_xattn_b_q"][by_d]
    wk, bk = f["L0_xattn_w_k"][by_d], f["L0_xattn_b_k"][by_d]

    def all_rows(routed, shared, first):
        a = np.concatenate([routed, shared[None]], 0)
        a = np.moveaxis(a, 0, first).reshape(*([D] if first else []), ROWS)
        return np.pad(a, [(0, 0)] * (a.ndim - 1) + [(0, TILES * P - ROWS)])

    w1 = all_rows(f["L0_ffn_w1"], f["L0_ffn_sw1"], 1)
    w3 = all_rows(f["L0_ffn_w3"], f["L0_ffn_sw3"], 1)
    w2 = np.zeros((TILES * P, D), np.float32)
    w2[:ROWS] = np.concatenate([f["L0_ffn_w2"].reshape(-1, D), f["L0_ffn_sw2"]])
    bias = (TILES - 1) * P + BIAS_ROW
    w2[bias:bias + E + 1] = np.concatenate([f["L0_ffn_b2"], f["L0_ffn_sb2"][None]])
    w2 = w2.reshape(TILES, P, D).transpose(1, 0, 2).reshape(P, TILES * D)
    is_bias = np.zeros(TILES * P, np.float32)
    is_bias[bias:bias + E + 1] = 1
    ecols = np.stack([all_rows(f["L0_ffn_b1"], f["L0_ffn_sb1"], 0), all_rows(f["L0_ffn_b3"], f["L0_ffn_sb3"], 0),
                      is_bias])
    def everywhere(*rows):
        return np.broadcast_to(np.concatenate(rows)[None], (P, sum(map(len, rows))))

    arrays = {
        "xc": np.concatenate([x, ctx.transpose(0, 2, 1)], 2),
        "mk": np.concatenate([mask, mask.transpose(0, 2, 1)], 2),
        "wqkvo": np.concatenate([wq.T, wk.T, f["L0_xattn_w_v"].T, f["L0_xattn_w_out"].T], 1),
        "cols": np.concatenate([np.stack([bq, bk, f["L0_xattn_b_v"]], 1), everywhere(f["g_xattn"], f["g_ffn"])], 1),
        "rows": everywhere(f["L0_xattn_b_out"], f["L0_ffn_gate_b"], np.arange(E, 0, -1, dtype=np.float32)),
        "gate_w": f["L0_ffn_gate_w"].T,
        "ident": np.eye(P, dtype=np.float32),
        "experts": np.stack([w1, w3, w2], 1),
        "expert_cols": ecols.reshape(3, TILES, P).transpose(2, 0, 1),
    }
    arrays = {name: np.ascontiguousarray(a) for name, a in arrays.items()}
    nc = bacc.Bacc("TRN2", target_bir_lowering=False, num_devices=1)
    aps = {name: nc.dram_tensor(name, a.shape, mybir.dt.from_np(a.dtype), kind="ExternalInput").ap()
           for name, a in arrays.items()}
    out = nc.dram_tensor("out", (B * P, D), F32, kind="ExternalOutput").ap()
    build(nc, out=out, **aps)
    r = run_bass_kernel_spmd(nc, [arrays], core_ids=[0])
    return r.results[0]["out"].reshape(B, P, D)
```
